# Optimizing a Trainium2 kernel written in Bass

```python
import numpy as np
import jax
import jax.numpy as jnp

def _softmax(x, axis=-1):
    return jax.nn.softmax(x, axis=axis)

def _gelu(x):
    return jax.nn.gelu(x, approximate=True)

def _silu(x):
    return jax.nn.silu(x)

def _sigmoid(x):
    return jax.nn.sigmoid(x)

def _layernorm(x, axis=-1, eps=1e-05):
    m = jnp.mean(x, axis=axis, keepdims=True)
    v = jnp.var(x, axis=axis, keepdims=True)
    return (x - m) / jnp.sqrt(v + eps)

def _scatter_add(tgt, idx, src, axis=0):
    return tgt.at[idx].add(src)

def _segment_sum(src, seg, n):
    return jax.ops.segment_sum(src, seg, n)
kernel_name = 'mk_adaln_ffn_d1_seqx_r4_16efc7'

def setup_inputs(seed: int=0):
    np.random.seed(seed)
    _w = jnp.asarray

    def _rec_inputs():
        import jax
        import jax.numpy as jnp
        _rk = jax.random.key(seed)
        x = -7.109e-05 + 0.9999 * jax.random.normal(jax.random.fold_in(_rk, 1), (16, 256, 512), jnp.float32)
        _lenS = 256 - jax.random.randint(jax.random.fold_in(_rk, 7), (16,), 0, max(1, 256 // 4) + 1, jnp.int32)
        _lenS2 = 256 - jax.random.randint(jax.random.fold_in(_rk, 8), (16,), 0, max(1, 256 // 4) + 1, jnp.int32)
        itok_B_0_6 = jax.random.randint(jax.random.fold_in(_rk, 11), (16,), 0, 7, jnp.int32)
        return (x, itok_B_0_6)
    x, itok_B_0_6 = _rec_inputs()

    def _L0_cond_setup():
        import jax, jax.numpy as jnp
        import numpy as np
        B, T, D_IN, D_OUT = (16, 512, 512, 512)
        N_ADAPTERS, RANK = (8, 16)
        key = jax.random.key(seed)
        k_x, k_w, k_a, k_b, k_s, k_idx = jax.random.split(key, 6)
        x = jax.random.normal(k_x, (B, T, D_IN), dtype=jnp.float32)
        W = jax.random.normal(k_w, (D_OUT, D_IN), dtype=jnp.float32) * (1.0 / np.sqrt(D_IN))
        A = jax.random.normal(k_a, (N_ADAPTERS, RANK, D_IN), dtype=jnp.float32) * 0.02
        Bm = jax.random.normal(k_b, (N_ADAPTERS, D_OUT, RANK), dtype=jnp.float32) * 0.02
        scalings = jnp.ones((N_ADAPTERS,), dtype=jnp.float32)
        adapter_idx = jax.random.randint(k_idx, (B,), 0, N_ADAPTERS, dtype=jnp.int32)
        return {'x': x, 'W': W, 'A': A, 'Bm': Bm, 'scalings': scalings, 'adapter_idx': adapter_idx}
    _L0_cond_all = _L0_cond_setup()
    _L0_cond_in = {k: v for k, v in _L0_cond_all.items() if k in ('W', 'A', 'Bm', 'scalings')}
    del _L0_cond_all

    def _L0_ffn_setup():
        import jax, jax.numpy as jnp
        import numpy as np
        E = 8
        TOP_K = 2
        D = 512
        DE = 352
        DS = 704
        B, S = (2, 512)
        key = jax.random.key(seed)
        ks = jax.random.split(key, 8)
        std = 0.02
        return {'x': jax.random.normal(ks[0], (B, S, D), jnp.float32), 'W_router': jax.random.normal(ks[1], (D, E), jnp.float32) * std, 'We_gate': jax.random.normal(ks[2], (E, D, DE), jnp.float32) * std, 'We_up': jax.random.normal(ks[3], (E, D, DE), jnp.float32) * std, 'We_down': jax.random.normal(ks[4], (E, DE, D), jnp.float32) * std, 'Ws_gate': jax.random.normal(ks[5], (D, DS), jnp.float32) * std, 'Ws_up': jax.random.normal(ks[6], (D, DS), jnp.float32) * std, 'Ws_down': jax.random.normal(ks[7], (DS, D), jnp.float32) * std}
    _L0_ffn_all = _L0_ffn_setup()
    _L0_ffn_in = {k: v for k, v in _L0_ffn_all.items() if k in ('W_router', 'We_gate', 'We_up', 'We_down', 'Ws_gate', 'Ws_up', 'Ws_down')}
    del _L0_ffn_all
    return {'x': x, 'itok_B_0_6': itok_B_0_6, 'L0_cond_W': _L0_cond_in['W'], 'L0_cond_A': _L0_cond_in['A'], 'L0_cond_Bm': _L0_cond_in['Bm'], 'L0_cond_scalings': _L0_cond_in['scalings'], 'L0_ffn_W_router': _L0_ffn_in['W_router'], 'L0_ffn_We_gate': _L0_ffn_in['We_gate'], 'L0_ffn_We_up': _L0_ffn_in['We_up'], 'L0_ffn_We_down': _L0_ffn_in['We_down'], 'L0_ffn_Ws_gate': _L0_ffn_in['Ws_gate'], 'L0_ffn_Ws_up': _L0_ffn_in['Ws_up'], 'L0_ffn_Ws_down': _L0_ffn_in['Ws_down']}

def reference(x, itok_B_0_6, L0_cond_W, L0_cond_A, L0_cond_Bm, L0_cond_scalings, L0_ffn_W_router, L0_ffn_We_gate, L0_ffn_We_up, L0_ffn_We_down, L0_ffn_Ws_gate, L0_ffn_Ws_up, L0_ffn_Ws_down):
    import jax
    import jax.numpy as jnp

    def _L0_cond_ref(x, W, A, Bm, scalings, adapter_idx):
        import jax, jax.numpy as jnp
        import numpy as np
        B, T, D_IN, D_OUT = (16, 512, 512, 512)
        N_ADAPTERS, RANK = (8, 16)
        H = jnp.einsum('btd,od->bto', x, W)
        A_b = A[adapter_idx]
        B_b = Bm[adapter_idx]
        s_b = scalings[adapter_idx]
        xa = jnp.einsum('btd,brd->btr', x, A_b)
        delta = jnp.einsum('btr,bor->bto', xa, B_b)
        delta = jax.lax.stop_gradient(delta * s_b[:, None, None])
        return H + delta

    def _L0_ffn_ref(x, W_router, We_gate, We_up, We_down, Ws_gate, Ws_up, Ws_down):
        import jax, jax.numpy as jnp
        import numpy as np
        E = 8
        TOP_K = 2
        D = 512
        DE = 352
        DS = 704
        B, S = (2, 512)
        b, s, d = x.shape
        shared = jax.nn.silu(x @ Ws_gate) * (x @ Ws_up) @ Ws_down
        scores = jax.nn.softmax(x @ W_router, axis=-1)
        topk_vals, topk_idx = jax.lax.top_k(scores, TOP_K)
        onehot = jax.nn.one_hot(topk_idx, E, dtype=x.dtype)
        combine = jnp.einsum('bsk,bske->bse', topk_vals, onehot)
        combine = combine.reshape(b * s, E)
        xf = x.reshape(b * s, d)
        h = jax.nn.silu(jnp.einsum('td,edh->eth', xf, We_gate)) * jnp.einsum('td,edh->eth', xf, We_up)
        y_all = jnp.einsum('eth,ehd->etd', h, We_down)
        routed = jnp.einsum('etd,te->td', y_all, combine)
        return routed.reshape(b, s, d) + shared
    x = x + _L0_ffn_ref(_L0_cond_ref(x, L0_cond_W, L0_cond_A, L0_cond_Bm, L0_cond_scalings, itok_B_0_6), L0_ffn_W_router, L0_ffn_We_gate, L0_ffn_We_up, L0_ffn_We_down, L0_ffn_Ws_gate, L0_ffn_Ws_up, L0_ffn_Ws_down)
    return x

_drawn_inputs = setup_inputs


def setup_inputs(seed=0):
    import zlib

    import numpy as np

    out = dict(_drawn_inputs(seed))
    spreads = {'L0_cond_scalings': (1.0, 0.6)}
    factors = {'L0_cond_A': 8.0,
     'L0_cond_Bm': 8.0,
     'L0_ffn_W_router': 4.227,
     'L0_ffn_We_gate': 3.823,
     'L0_ffn_We_up': 3.716,
     'L0_ffn_We_down': 3.703}
    for name, (base, spread) in spreads.items():
        noise = np.random.default_rng([zlib.crc32(name.encode()), seed]).standard_normal(out[name].shape)
        drawn = base * np.exp(spread * noise) if base else spread * noise
        out[name] = jnp.asarray(drawn.astype(out[name].dtype))
    for name, factor in factors.items():
        out[name] = (out[name] * factor).astype(out[name].dtype)
    return out
```

```python
from contextlib import ExitStack

import concourse.bass as bass
from concourse import mybir

F32, F16, I32 = mybir.dt.float32, mybir.dt.float16, mybir.dt.int32
ALU = mybir.AluOpType
ACT = mybir.ActivationFunctionType
AX = mybir.AxisListType.X

P = 128
HI, LO = 0, 1
GATE, UP, DOWN = 0, 1, 2

EXP_MASK = 0x7F800000
ONE_EXP = 1 << 23
TOP = 14
MIN_EXP = 27


def adaln_moe_kernel(nc, x, adapter_idx, cond_w, lora_a, lora_b, scalings, w_router,
                     we_gate, we_up, we_down, ws_gate, ws_up, ws_down, out):
    B, S, D = x.shape
    NA, RANK, _ = lora_a.shape
    E, _, H = we_gate.shape
    assert NA * RANK == P and ws_gate.shape[1] == 2 * H and D == 4 * P
    TOKENS = B * S
    T = TOKENS // P
    TPB = S // P
    KD = D // P
    KH = -(-H // P)
    HR = H - (KH - 1) * P
    EX = E + 2
    ET = 2 * TOKENS // P + E - 1
    S1T = 9
    N1 = 2 * S1T
    N2 = N1 + ET
    NS = N2 + 2 * (T - S1T)
    H1 = S1T
    H2 = H1 + ET
    SLOTS = (ET + 1) * P
    assert TPB == 2 and ET % 2 == 1 and S1T % 2 == 1 and (T - S1T) % 2 == 1 and N1 % 2 == 0

    x_rows = x.rearrange("b (t p) d -> (b t) p d", p=P)
    out_rows = out.rearrange("b (t p) d -> (b t) p d", p=P)
    h_dram = nc.dram_tensor("h_dram", [TOKENS, D], F32).ap()
    y_dram = nc.dram_tensor("y_dram", [ET * P, D], F32).ap()
    part_dram = nc.dram_tensor("part_dram", [S1T * P, D], F32).ap()
    meta_dram = nc.dram_tensor("meta_dram", [SLOTS, 4], F32).ap()
    h_tiles = h_dram.rearrange("(t p) d -> t p d", p=P)
    y_tiles = y_dram.rearrange("(t p) d -> t p d", p=P)
    part_tiles = part_dram.rearrange("(t p) d -> t p d", p=P)
    ds = bass.ds

    with ExitStack() as ctx:
        def sb(name, shape, dt, c=ctx):
            return c.enter_context(nc.sbuf_tensor(name, shape, dt))

        def sem(name):
            return ctx.enter_context(nc.semaphore(name))

        wg = sb("wg", [P, EX, KD, 2, H], F16)
        wu = sb("wu", [P, EX, KD, 2, H], F16)
        wd = sb("wd", [P, EX, KH, 2, D], F16)
        ident = sb("ident", [P, P], F32)
        ch = sb("ch", [P, T], F32)
        winv = sb("winv", [P, 3, EX], F32)
        logits = sb("logits", [P, T, E], F32)
        iota_e = sb("iota_e", [P, E], F32)
        iota_j = sb("iota_j", [P, ET], F32)

        actx = ExitStack()
        cw = sb("cw", [P, KD, 2, D], F16, actx)
        lat = sb("lat", [P, KD, 2, P], F16, actx)
        lbt = sb("lbt", [P, D], F32, actx)
        wr = sb("wr", [P, KD, 2, E], F16, actx)
        lmask = sb("lmask", [P, B], F32, actx)
        stage = sb("stage", [P, 2, KH * D], F32, actx)
        xrow = sb("xrow", [P, 2, D], F32, actx)
        xt = sb("xt", [P, 2, 2, KD, P], F16, actx)
        xam = sb("xam", [P, P], F32, actx)
        hs = sb("hs", [P, D], F32, actx)
        xinv = sb("xinv", [P, T], F32, actx)
        small = sb("small", [P, 16], F32, actx)
        rlog = sb("rlog", [P, 2, E], F32, actx)
        pcol = sb("pcol", [P, 4], F32, actx)
        rexp = sb("rexp", [P, 3, 4], F32, actx)
        wr32 = sb("wr32", [P, KD, E], F32, actx)
        actx.close()

        hin = sb("hin", [P, 2, D], F32)
        ht = sb("ht", [P, 2, 2, KD, P], F16)
        act = sb("act", [P, H], F32)
        at = sb("at", [P, 2, 2, KH, P], F16)
        acc = sb("acc", [P, 2, D], F32)
        cg = sb("cg", [P, NS], F32)
        cu = sb("cu", [P, NS], F32)
        cd = sb("cd", [P, NS], F32)
        cy = sb("cy", [P, NS], F32)
        fsm = sb("fsm", [P, 4], F32)
        meta = sb("meta", [P, ET, 4], F32)
        idx = sb("idx", [P, 2], I32)
        pos = sb("pos", [P, T, 2], I32)
        posb = sb("posb", [P, 4], I32)
        etile = sb("etile", [P, ET], I32)
        route = sb("route", [P, 3072], F32)
        yout = route[:, 0:2 * D].rearrange("p (b d) -> p b d", b=2)
        gat = route[:, 2 * D:6 * D].rearrange("p (b s d) -> p b s d", b=2, s=2)

        at_ = [0]

        def take(n):
            at_[0] += n
            return route[:, at_[0] - n:at_[0]]

        def te(v):
            return v.rearrange("p (t e) -> p t e", e=E)

        TE = T * E
        r_s, r_eq, r_cand = take(TE), take(TE), take(TE)
        r_oh1, r_oh2 = take(TE), take(TE)
        r_s2, r_cs, r_in0, r_in1 = take(TE), take(TE), take(TE), take(TE)
        pay = take(TE).rearrange("p (t s c) -> p t s c", s=2, c=4)
        m16 = take(TE // 2).bitcast(F16)
        upper16, ones16 = take(P // 2).bitcast(F16), take(P // 2).bitcast(F16)
        r_max, r_sum, r_v1, r_e1, r_v2, r_e2 = [take(T) for _ in range(6)]
        r_n, r_tiles, r_end, r_base, r_tmp = [take(E) for _ in range(5)]
        assert at_[0] <= 3072 and ET * E <= 3 * TE
        j_a = route[:, 0:ET * E].rearrange("p (j e) -> p j e", e=E)
        j_b = route[:, 5 * TE:5 * TE + ET * E].rearrange("p (j e) -> p j e", e=E)

        ps = ctx.enter_context(nc.psum_tensor("ps", [P, 8, 512], F32))
        p_tx, p_th, p_xa, p_rt = ps[:, 0, :], ps[:, 1, :], ps[:, 2, 0:P], ps[:, 3, 0:2 * E]
        p_h = [ps[:, 4, :], ps[:, 5, :]]
        p_rank, p_count = ps[:, 6, 0:TE], ps[:, 7, 0:TE]
        p_fth, p_at = ps[:, 0, :], ps[:, 1, :]
        p_g = [ps[:, 2, 0:H], ps[:, 3, 0:H]]
        p_u = [ps[:, 4, 0:H], ps[:, 5, 0:H]]
        p_y = [ps[:, 6, :], ps[:, 7, :]]

        s_const = sem("s_const")
        s_pin = sem("s_pin")
        s_pmx = sem("s_pmx")
        s_par = sem("s_par")
        s_pc = sem("s_pc")
        s_pt = sem("s_pt")
        s_phi = sem("s_phi")
        s_plo = sem("s_plo")
        s_z = sem("s_z")
        s_meta0 = sem("s_meta0")
        s_xld = [sem("s_xld0"), sem("s_xld1")]
        s_xmx, s_xex, s_xiv, s_xsc, s_xs = sem("s_xmx"), sem("s_xex"), sem("s_xiv"), sem("s_xsc"), sem("s_xs")
        s_tx, s_xhi, s_xlo = sem("s_tx"), sem("s_xhi"), sem("s_xlo")
        s_xa, s_xam, s_h = sem("s_xa"), sem("s_xam"), sem("s_h")
        s_hmx, s_hex, s_hiv, s_hsc, s_hs = sem("s_hmx"), sem("s_hex"), sem("s_hiv"), sem("s_hsc"), sem("s_hs")
        s_ch, s_hst = sem("s_ch"), sem("s_hst")
        s_th, s_hhi, s_hlo = sem("s_th"), sem("s_hhi"), sem("s_hlo")
        s_rt, s_rlog, s_log = sem("s_rt"), sem("s_rlog"), sem("s_log")
        s_wld = [sem("s_wld0"), sem("s_wld1")]
        s_pad, s_wmx, s_war = sem("s_pad"), sem("s_wmx"), sem("s_war")
        s_wex, s_wiv, s_wsc, s_whi, s_wfree = sem("s_wex"), sem("s_wiv"), sem("s_wsc"), sem("s_whi"), sem("s_wfree")
        s_r = sem("s_r")
        s_rd, s_re, s_m16, s_rmm = sem("s_rd"), sem("s_re"), sem("s_m16"), sem("s_rmm")
        s_pay, s_scat, s_metain, s_et = sem("s_pay"), sem("s_scat"), sem("s_metain"), sem("s_et")
        s_coef = sem("s_coef")
        s_hin = [sem("s_hin0"), sem("s_hin1")]
        s_hgat = [sem("s_hgat0"), sem("s_hgat1")]
        s_fth, s_fhi, s_flo = sem("s_fth"), sem("s_fhi"), sem("s_flo")
        s_gu, s_silu, s_a = sem("s_gu"), sem("s_silu"), sem("s_a")
        s_amx, s_aex, s_aiv, s_asc, s_as, s_cy = (sem("s_amx"), sem("s_aex"), sem("s_aiv"), sem("s_asc"),
                                                  sem("s_as"), sem("s_cy"))
        s_ta, s_ahi, s_alo, s_dn = sem("s_ta"), sem("s_ahi"), sem("s_alo"), sem("s_dn")
        s_y = sem("s_y")
        s_yst = [sem("s_yst0"), sem("s_yst1")]
        s_xin = [sem("s_xin0"), sem("s_xin1")]
        s_acc = sem("s_acc")
        s_pst = [sem("s_pst0"), sem("s_pst1")]
        s_ix = sem("s_ix")
        s_g = [sem("s_g0"), sem("s_g1")]
        s_pld = [sem("s_pld0"), sem("s_pld1")]
        s_add = sem("s_add")
        s_out = [sem("s_out0"), sem("s_out1")]

        block = ctx.enter_context(nc.Block())

        def tval(c, i, k=0, per=6):
            return c + k if i is None else c + k + i * per

        def chunk(c, i):
            return c % 3, tval(c // 3, i, 0, 2)

        QN = 3 * EX

        class Slot:
            def __init__(s, c, i=None):
                shared = c < N1 or c >= N2
                per = 4 if shared else 2
                s.i = i
                s.c, s.n, s.par = c, tval(c, i, 0, per), c % 2
                s.shared = shared
                if shared:
                    m = c if c < N1 else c - N2
                    tile = m // 2 if c < N1 else S1T + m // 2
                    s.half = m % 2
                    s.hc = m // 2 if c < N1 else H2 + m // 2
                    s.h, s.tile, s.tpar = tval(s.hc, i, 0, 2), tval(tile, i, 0, 2), tile % 2
                    s.tq = tval(tile // 2, i, 0, 1)
                    s.first = c < N1
                    s.expert = E + s.half
                    s.last = s.half == 1
                    s.k = tval(m if c < N1 else c - ET, i, 0, 4)
                else:
                    s.hc = H1 + c - N1
                    s.h, s.j, s.last = tval(s.hc, i, 0, 2), tval(c - N1, i, 0, 2), True
                s.hpar = s.hc % 2

        def run_slots(eng, do):
            def straight(c):
                do(Slot(c), Slot(c - 1) if c else None)

            def loop(start, count, per):
                with eng.Fori(0, count) as i:
                    for c in range(start, start + per):
                        prev = Slot(c - 1, i)
                        do(Slot(c, i), prev)
            for start, end, per in ((0, N1, 4), (N1, N2, 2), (N2, NS, 4)):
                for c in range(start, start + 3):
                    straight(c)
                count = (end - start - 4) // per
                loop(start + 3, count, per)
                for c in range(start + 3 + count * per, end):
                    straight(c)

        def tail(do):
            do(None, Slot(NS - 1))

        def yst_before(s):
            return (s.c - N1) // 2 * 16 if isinstance(s.j, int) else (s.j - (s.c - N1)) * 8 + (s.c - N1) // 2 * 16

        def col(table, n):
            return table[:, n:n + 1] if isinstance(n, int) else table[:, ds(n, 1)]

        def w_views(c, i, half):
            kind, e = chunk(c, i)
            w = (wg, wu, wd)[kind]
            k, n = (KH, D) if kind == DOWN else (KD, H)
            dst = w[:, e, :, half, :] if isinstance(e, int) else \
                w[:, ds(e, 1), :, half, :].rearrange("p a k n -> p (a k) n")
            return dst, stage[:, c % 2, 0:k * n].rearrange("p (k n) -> p k n", k=k)

        @block.sync
        def _(sp):
            w_src = stage[:, :, :].rearrange("p b n -> p (b n)")
            sp.dma_start(w_src[:, 0:KD * D].rearrange("p (c d) -> p c d", c=KD),
                         cond_w.rearrange("(c p) d -> p c d", p=P)).then_inc(s_pin, 16)
            sp.dma_start(w_src[:, KD * D:KD * D + D], lora_a.rearrange("a r d -> (a r) d")).then_inc(s_pin, 16)
            for a in range(NA):
                sp.dma_start(
                    w_src[:, KD * D + D:KD * D + 2 * D].rearrange("p (c a r) -> p c a r", c=KD, a=NA)[:, :, a, :],
                    lora_b[a].rearrange("(c p) r -> p c r", p=P)).then_inc(s_pin, 16)
            sp.dma_start(wr32[:, :, :], w_router.rearrange("(k p) e -> p k e", p=P)).then_inc(s_pin, 16)
            sp.dma_start(lmask[:, :].bitcast(I32), adapter_idx.partition_broadcast(P)).then_inc(s_pin, 16)
            for a in range(NA):
                sp.dma_start(pcol[a * RANK:(a + 1) * RANK, 0:1],
                             scalings[a:a + 1].partition_broadcast(RANK)).then_inc(s_pin, 16)

            def load_x(c, i):
                t = tval(c, i)
                if c >= 2:
                    sp.wait_ge(s_tx, tval(c, i, -1))
                src = x_rows[t] if i is None else x_rows[ds(t, 1)].rearrange("a p d -> (a p) d")
                sp.dma_start(xrow[:, c % 2, :], src).then_inc(s_xld[c % 2], 16)

            def load_w(c, i):
                q = tval(c, i)
                kind, e = chunk(c, i)
                sp.wait_ge(s_wfree, tval(c, i, 1))
                if i is None and e >= E:
                    half = e - E
                    src = [ws_gate[:, half * H:(half + 1) * H], ws_up[:, half * H:(half + 1) * H],
                           ws_down[half * H:(half + 1) * H, :]][kind]
                else:
                    src = [we_gate, we_up, we_down][kind]
                    src = src[e] if i is None else src[ds(e, 1)].rearrange("a r n -> (a r) n")
                dst = stage[:, c % 2, :]
                if kind == DOWN:
                    whole = (KH - 1) * P
                    sp.dma_start(dst[:, 0:(KH - 1) * D].rearrange("p (k d) -> p k d", d=D),
                                 src[0:whole, :].rearrange("(k p) d -> p k d", p=P)).then_inc(s_wld[c % 2], 16)
                    sp.dma_start(dst[0:HR, (KH - 1) * D:KH * D], src[whole:H, :]).then_inc(s_wld[c % 2], 16)
                else:
                    sp.dma_start(dst[:, 0:KD * H].rearrange("p (k h) -> p k h", h=H),
                                 src.rearrange("(k p) h -> p k h", p=P)).then_inc(s_wld[c % 2], 16)

            def store_h(c, i):
                t = tval(c, i)
                sp.wait_ge(s_hs, tval(c, i, 1))
                dst = h_tiles[t] if i is None else h_tiles[ds(t, 1)].rearrange("a p d -> (a p) d")
                sp.dma_start(dst, hs[:, :]).then_inc(s_hst, 16)

            def step(c, i=None):
                if 0 <= c - 1 < T:
                    store_h(c - 1, i)
                if 0 <= c + 2 < T:
                    load_x(c + 2, i)
                if 0 <= c - 2 < QN:
                    load_w(c - 2, i)

            for c in range(-2, 2):
                step(c)
            with sp.Fori(0, 4) as i:
                for c in range(2, 8):
                    step(c, i)
            for c in range(26, T + 1):
                step(c)

            sp.wait_ge(s_hst, 16 * T)
            sp.wait_ge(s_log, T)
            sp.wait_ge(s_wfree, QN + 2)

            def load_h(s):
                if s.c >= 2 * 2 or not s.first:
                    sp.wait_ge(s_fth, s.h - 1)
                src = h_tiles[s.tile] if isinstance(s.tile, int) else h_tiles[ds(s.tile, 1)].rearrange("a p d -> (a p) d")
                sp.dma_start(hin[:, s.hpar, :], src).then_inc(s_hin[s.hpar], 16)

            def load_acc(s):
                if s.first and s.c >= 4:
                    sp.wait_ge(s_pst[s.tpar], s.tq * 16)
                elif not s.first:
                    if s.c < N2 + 4:
                        sp.wait_ge(s_pst[s.tpar], s.tq * 16)
                    else:
                        sp.wait_ge(s_out[s.tpar], s.tq * 16)
                src = x_rows[s.tile] if isinstance(s.tile, int) else x_rows[ds(s.tile, 1)].rearrange("a p d -> (a p) d")
                sp.dma_start(acc[:, s.tpar, :], src).then_inc(s_xin[s.tpar], 16)

            def store_part(s):
                sp.wait_ge(s_acc, s.k + 1)
                dst = part_tiles[s.tile] if isinstance(s.tile, int) else part_tiles[ds(s.tile, 1)].rearrange("a p d -> (a p) d")
                sp.dma_start(dst, acc[:, s.tpar, :]).then_inc(s_pst[s.tpar], 16)

            def store_y(s):
                sp.wait_ge(s_y, s.j + 1)
                dst = y_tiles[s.j] if isinstance(s.j, int) else y_tiles[ds(s.j, 1)].rearrange("a p d -> (a p) d")
                sp.dma_start(dst, yout[:, s.par, :]).then_inc(s_yst[s.par], 16)

            for t in range(2):
                load_h(Slot(2 * t))
                load_acc(Slot(2 * t))
            store_part(Slot(1))
            load_h(Slot(4))
            load_acc(Slot(4))
            with sp.Fori(0, (S1T - 3) // 2) as i:
                for t in range(1, 3):
                    store_part(Slot(2 * t + 1, i))
                    load_h(Slot(2 * t + 4, i))
                    load_acc(Slot(2 * t + 4, i))
            sp.wait_ge(s_scat, 16 * 2 * T)
            sp.dma_start(meta[:, :, :], meta_dram[0:ET * P, :].rearrange("(j p) c -> p j c", p=P)).then_inc(s_metain, 16)
            for t in range(S1T - 2, S1T):
                store_part(Slot(2 * t + 1))
            with sp.Fori(0, (ET - 3) // 2) as i:
                for c in range(N1, N1 + 2):
                    store_y(Slot(c, i))
            load_h(Slot(N2))
            load_acc(Slot(N2))
            store_y(Slot(N2 - 3))
            load_h(Slot(N2 + 2))
            load_acc(Slot(N2 + 2))
            store_y(Slot(N2 - 2))
            store_y(Slot(N2 - 1))
            load_h(Slot(N2 + 4))
            load_acc(Slot(N2 + 4))
            with sp.Fori(0, (T - S1T - 3) // 2) as i:
                for c in (N2 + 6, N2 + 8):
                    load_h(Slot(c, i))
                    load_acc(Slot(c, i))

        @block.gpsimd
        def _(pool):
            pool.memset(ident[:, :], 0.0).then_inc(s_z, 1)
            pool.wait_ge(s_z, 1)
            pool.affine_select(out=ident[:, :], in_=ident[:, :], compare_op=ALU.not_equal, fill=1.0, base=0,
                               pattern=[[-1, P]], channel_multiplier=1).then_inc(s_const, 1)
            pool.iota(iota_e[:, :], [[1, E]], base=0, channel_multiplier=0,
                      allow_small_or_imprecise_dtypes=True).then_inc(s_const, 1)
            pool.iota(iota_j[:, :], [[1, ET]], base=0, channel_multiplier=0,
                      allow_small_or_imprecise_dtypes=True).then_inc(s_const, 1)
            pool.iota(pcol[:, 1:2].bitcast(I32), [[0, 1]], base=0, channel_multiplier=1).then_inc(s_const, 1)
            pool.memset(hs[:, 0:SLOTS * 4 // P], 0.0).then_inc(s_z, 1)
            pool.wait_ge(s_z, 2)
            pool.dma_start(meta_dram.rearrange("(p j) c -> p (j c)", p=P), hs[:, 0:SLOTS * 4 // P]).then_inc(s_meta0, 16)
            pool.wait_ge(s_pmx, 3)
            pool.partition_all_reduce(rexp[:, 0, 0:3], small[:, 0:3], P, bass.bass_isa.ReduceOp.max).then_inc(s_par, 1)

            def pad(c, i):
                pool.wait_ge(s_wfree, tval(c, i, 1))
                pool.nop(nofuse=True)
                pool.memset(stage[HR:P, c % 2, (KH - 1) * D:KH * D], 0.0).then_inc(s_pad, 1)

            def step(c, i=None):
                if c % 3 == 1:
                    pad(c + 1, i)
                    pool.wait_ge(s_pad, tval(c // 3, i, 1, 2))
                pool.wait_ge(s_wmx, tval(c, i, 1))
                pool.nop(nofuse=True)
                pool.partition_all_reduce(small[:, 13:14], small[:, 12:13], P,
                                          bass.bass_isa.ReduceOp.max).then_inc(s_war, 1)

            with pool.Fori(0, 4) as i:
                for c in range(6):
                    step(c, i)
            for c in range(24, QN):
                step(c)

            pool.wait_ge(s_log, T)
            pool.wait_ge(s_hst, 16 * T)
            pool.wait_ge(s_wfree, QN + 2)
            pool.memset(ones16, 1.0).then_inc(s_z, 1)
            pool.wait_ge(s_z, 3)
            pool.affine_select(out=upper16, in_=ones16, compare_op=ALU.is_gt, fill=0.0, base=0,
                               pattern=[[1, P]], channel_multiplier=-1).then_inc(s_const, 1)
            pool.iota(pay[:, :, :, 0].bitcast(I32), [[P, T], [0, 2]], base=0, channel_multiplier=1).then_inc(s_const, 1)
            pool.memset(pay[:, :, :, 3], 0.0).then_inc(s_const, 1)
            pool.wait_ge(s_meta0, 16)
            pool.wait_ge(s_const, 7)
            pool.wait_ge(s_pay, 2)
            for t in range(T):
                for k in range(2):
                    pool.indirect_dma_start(
                        out=meta_dram, out_offset=bass.IndirectOffsetOnAxis(ap=pos[:, t, k:k + 1], axis=0),
                        in_=pay[:, t, k, :], in_offset=None).then_inc(s_scat, 16)
            pool.wait_ge(s_metain, 16)
            pool.wait_ge(s_hst, 16 * T)

            def gather_h(s):
                pool.wait_ge(s_fth, s.h - 1)
                col = meta[:, s.j, 0:1] if isinstance(s.j, int) else \
                    meta[:, ds(s.j, 1), 0:1].rearrange("p a c -> p (a c)")
                pool.tensor_copy(idx[:, s.hpar:s.hpar + 1], col.bitcast(I32)).then_inc(s_ix, 1)
                pool.wait_ge(s_ix, s.j + 1)
                pool.nop(nofuse=True)
                pool.indirect_dma_start(
                    out=hin[:, s.hpar, :], out_offset=None, in_=h_dram,
                    in_offset=bass.IndirectOffsetOnAxis(ap=idx[:, s.hpar:s.hpar + 1], axis=0)
                ).then_inc(s_hgat[s.hpar], 16)

            gather_h(Slot(N1))
            with pool.Fori(0, (ET - 1) // 2) as i:
                for c in range(N1 + 1, N1 + 3):
                    gather_h(Slot(c, i))

            pool.wait_ge(s_yst[0], 16 * ((ET + 1) // 2))
            pool.wait_ge(s_yst[1], 16 * (ET // 2))

            def finish(tc, i, before, early):
                b = tc % 2
                t = tval(tc, i, 0, 2)
                done = tval(tc, i, 0, 2)
                if early:
                    if tc >= 2:
                        pool.wait_ge(s_out[b], tval(tc // 2, i, 0, 1) * 16)
                        pool.nop(nofuse=True)
                    src = part_tiles[t] if i is None else part_tiles[ds(t, 1)].rearrange("a p d -> (a p) d")
                    pool.dma_start(before, src).then_inc(s_pld[b], 16)
                for k in range(2):
                    col = pos[:, t, k:k + 1] if i is None else \
                        pos[:, ds(t, 1), k:k + 1].rearrange("p a c -> p (a c)")
                    pool.tensor_copy(posb[:, 2 * b + k:2 * b + k + 1], col).then_inc(s_ix, 1)
                pool.wait_ge(s_ix, ET + 2 + 2 * done)
                pool.nop(nofuse=True)
                for k in range(2):
                    pool.indirect_dma_start(
                        out=gat[:, b, k, :], out_offset=None, in_=y_dram,
                        in_offset=bass.IndirectOffsetOnAxis(ap=posb[:, 2 * b + k:2 * b + k + 1], axis=0)
                    ).then_inc(s_g[b], 16)
                pool.wait_ge(s_g[b], 32 + 32 * tval(tc // 2, i, 0, 1))
                if early:
                    pool.wait_ge(s_pld[b], 16 + 16 * tval(tc // 2, i, 0, 1))
                else:
                    pool.wait_ge(s_acc, 2 + 2 * t)
                pool.tensor_tensor(before, before, gat[:, b, 0, :], ALU.add).then_inc(s_add, 1)
                pool.wait_ge(s_add, 1 + 2 * done)
                pool.tensor_tensor(before, before, gat[:, b, 1, :], ALU.add).then_inc(s_add, 1)
                pool.wait_ge(s_add, 2 + 2 * done)
                pool.nop(nofuse=True)
                dst = out_rows[t] if i is None else out_rows[ds(t, 1)].rearrange("a p d -> (a p) d")
                pool.dma_start(dst, before).then_inc(s_out[b], 16)

            finish(0, None, yout[:, 0, :], True)
            finish(1, None, yout[:, 1, :], True)
            with pool.Fori(0, (S1T - 3) // 2) as i:
                for tc in (2, 3):
                    finish(tc, i, yout[:, tc % 2, :], True)
            finish(S1T - 1, None, yout[:, (S1T - 1) % 2, :], True)
            with pool.Fori(0, (T - S1T - 1) // 2) as i:
                for tc in (S1T, S1T + 1):
                    finish(tc, i, acc[:, tc % 2, :], False)
            finish(T - 1, None, acc[:, (T - 1) % 2, :], False)
            pool.wait_ge(s_out[0], 16 * (T // 2))
            pool.wait_ge(s_out[1], 16 * (T // 2))

        @block.scalar
        def _(a):
            a.wait_ge(s_pc, 2)
            for k in range(KD + 1):
                a.wait_ge(s_pt, k + 1)
                dst = cw[:, k, HI, :] if k < KD else lat[:, :, HI, :]
                src = ps[:, k, :] if k < KD else ps[:, k, :].rearrange("p (k n) -> p k n", k=KD)
                part = 0 if k < KD else 1
                nc.scalar.activation(dst, src, ACT.Copy, scale=rexp[:, 2, part:part + 1]).then_inc(s_phi, 1)
            a.wait_ge(s_pt, KD + 2)
            nc.scalar.activation(lbt[:, :], ps[:, KD + 1, :], ACT.Copy).then_inc(s_phi, 1)
            nc.scalar.activation(wr[:, :, HI, :], wr32[:, :, :], ACT.Copy, scale=rexp[:, 2, 2:3]).then_inc(s_phi, 1)

            def split_w(c, i):
                q = tval(c, i)
                kind, e = chunk(c, i)
                a.wait_ge(s_wsc, tval(c, i, 1))
                dst, src = w_views(c, i, HI)
                nc.scalar.activation(dst, src, ACT.Copy, scale=small[:, 15:16]).then_inc(s_whi, 1)

            def step(c, i=None):
                t = tval(c, i)
                if 0 <= c + 1 < T:
                    a.wait_ge(s_tx, tval(c, i, 2))
                    nc.scalar.activation(xt[:, (c + 1) % 2, HI, :, :], p_tx.rearrange("p (k n) -> p k n", k=KD),
                                         ACT.Copy).then_inc(s_xhi, 1)
                if 0 <= c < T:
                    a.wait_ge(s_xa, tval(c, i, 1))
                    b = tval(c // 2, i, 0, 3)
                    a.nop(nofuse=True)
                    m = lmask[:, b:b + 1] if i is None else lmask[:, ds(b, 1)]
                    nc.scalar.activation(xam[:, :], p_xa, ACT.Copy, scale=m).then_inc(s_xam, 1)
                if 0 <= c + 2 < T:
                    a.wait_ge(s_xsc, tval(c, i, 3))
                    nc.scalar.activation(xrow[:, c % 2, :], xrow[:, c % 2, :], ACT.Copy,
                                         scale=small[:, 2 + c % 2:3 + c % 2]).then_inc(s_xs, 1)
                if 0 <= c - 1 < T:
                    a.wait_ge(s_th, tval(c, i))
                    nc.scalar.activation(xt[:, c % 2, HI, :, :], p_th.rearrange("p (k n) -> p k n", k=KD),
                                         ACT.Copy).then_inc(s_hhi, 1)
                if 0 <= c - 3 < QN:
                    split_w(c - 3, i)
                if 0 <= c < T:
                    a.wait_ge(s_hsc, tval(c, i, 1))
                    if c >= 1:
                        a.wait_ge(s_hst, tval(c, i) * 16)
                    else:
                        a.wait_ge(s_meta0, 16)
                    nc.scalar.activation(hs[:, :], p_h[c % 2], ACT.Copy, scale=small[:, 7:8]).then_inc(s_hs, 1)

            for c in range(-2, 3):
                step(c)
            with a.Fori(0, 4) as i:
                for c in range(3, 9):
                    step(c, i)
            for c in range(27, T + 1):
                step(c)

            a.wait_ge(s_rd, 1)
            nc.scalar.activation(r_s, r_s, ACT.Exp).then_inc(s_re, 1)

            def slot(s, prev):
                if s and s.last and s.c < NS - 1:
                    a.wait_ge(s_fth, s.h + 2)
                    nc.scalar.activation(ht[:, 1 - s.hpar, HI, :, :], p_fth.rearrange("p (k n) -> p k n", k=KD),
                                         ACT.Copy).then_inc(s_fhi, 1)
                if prev:
                    a.wait_ge(s_ta, prev.n + 1)
                    nc.scalar.activation(at[:, prev.par, HI, :, :].rearrange("p k n -> p (k n)"), p_at[:, 0:KH * P],
                                         ACT.Copy).then_inc(s_ahi, 1)
                if s:
                    a.wait_ge(s_gu, s.n + 1)
                    if s.c == 0:
                        a.wait_ge(s_coef, 12)
                    if s.c == N1:
                        a.wait_ge(s_coef, 15)
                    nc.scalar.activation(act[:, :], p_g[s.par], ACT.Silu, scale=col(cg, s.n)).then_inc(s_silu, 1)
                    a.wait_ge(s_asc, s.n + 1)
                    nc.scalar.activation(act[:, :], act[:, :], ACT.Copy, scale=fsm[:, 2:3]).then_inc(s_as, 1)
                if prev and not prev.shared:
                    a.wait_ge(s_dn, prev.n + 1)
                    a.wait_ge(s_cy, prev.n + 1)
                    if prev.c >= N1 + 2:
                        a.wait_ge(s_yst[prev.par], yst_before(prev))
                    nc.scalar.activation(yout[:, prev.par, :], p_y[prev.par], ACT.Copy,
                                         scale=col(cy, prev.n)).then_inc(s_y, 1)

            a.wait_ge(s_fth, 1)
            nc.scalar.activation(ht[:, 0, HI, :, :], p_fth.rearrange("p (k n) -> p k n", k=KD), ACT.Copy).then_inc(s_fhi, 1)
            run_slots(a, slot)
            tail(slot)

        @block.vector
        def _(v):
            V = nc.vector

            def row_max(o, src, axis=AX):
                return V.tensor_reduce(o, src, axis, ALU.max, apply_absolute_value=True)

            def exponent(o, amax):
                return V.tensor_scalar(o.bitcast(I32), amax.bitcast(I32), EXP_MASK, None, ALU.bitwise_and)

            def inverse(o, ex):
                return V.tensor_scalar(o.bitcast(I32), ex.bitcast(I32), float(MIN_EXP * ONE_EXP),
                                       float(-TOP * ONE_EXP), ALU.max, ALU.add)

            def scale_of(o, inv):
                return V.tensor_scalar(o.bitcast(I32), inv.bitcast(I32), -1.0, float(254 * ONE_EXP),
                                       ALU.mult, ALU.add)

            v.wait_ge(s_pin, 16 * (2 + NA + 2 + NA))
            w_src = stage[:, :, :].rearrange("p b n -> p (b n)")
            row_max(small[:, 0:1], w_src[:, 0:KD * D]).then_inc(s_pmx, 1)
            row_max(small[:, 1:2], w_src[:, KD * D:KD * D + D]).then_inc(s_pmx, 1)
            row_max(small[:, 2:3], wr32[:, :, :].rearrange("p k e -> p (k e)")).then_inc(s_pmx, 1)
            v.wait_ge(s_par, 1)
            exponent(rexp[:, 1, 0:3], rexp[:, 0, 0:3]).then_inc(s_plo, 1)
            v.wait_ge(s_plo, 1)
            inverse(rexp[:, 1, 0:3], rexp[:, 1, 0:3]).then_inc(s_pc, 1)
            v.wait_ge(s_pc, 1)
            scale_of(rexp[:, 2, 0:3], rexp[:, 1, 0:3]).then_inc(s_pc, 1)
            v.wait_ge(s_const, 4)
            V.tensor_scalar(pcol[:, 1:2].bitcast(I32), pcol[:, 1:2].bitcast(I32), RANK.bit_length() - 1, None,
                            ALU.arith_shift_right).then_inc(s_pc, 1)
            V.tensor_copy(lmask[:, :], lmask[:, :].bitcast(I32)).then_inc(s_pc, 1)
            v.wait_ge(s_pc, 4)
            V.tensor_copy(pcol[:, 2:3], pcol[:, 1:2].bitcast(I32)).then_inc(s_pc, 1)
            V.tensor_scalar(pcol[:, 3:4], pcol[:, 0:1], rexp[:, 2, 0:1], rexp[:, 1, 1:2],
                            ALU.mult, ALU.mult).then_inc(s_pc, 1)
            v.wait_ge(s_pc, 6)
            V.tensor_scalar(lmask[:, :], lmask[:, :], pcol[:, 2:3], pcol[:, 3:4],
                            ALU.is_equal, ALU.mult).then_inc(s_pc, 1)
            for k in range(KD + 1):
                v.wait_ge(s_phi, k + 1)
                hi, lo = (cw[:, k, HI, :], cw[:, k, LO, :]) if k < KD else (lat[:, :, HI, :], lat[:, :, LO, :])
                src = ps[:, k, :] if k < KD else ps[:, k, :].rearrange("p (k n) -> p k n", k=KD)
                c_ = 0 if k < KD else 1
                V.scalar_tensor_tensor(out=lo, in0=src, scalar=rexp[:, 2, c_:c_ + 1], in1=hi,
                                       op0=ALU.mult, op1=ALU.subtract).then_inc(s_plo, 1)
            v.wait_ge(s_phi, KD + 3)
            V.scalar_tensor_tensor(out=wr[:, :, LO, :], in0=wr32[:, :, :], scalar=rexp[:, 2, 2:3],
                                   in1=wr[:, :, HI, :], op0=ALU.mult, op1=ALU.subtract).then_inc(s_plo, 1)

            def step(c, i=None):
                def tab(table, k):
                    n = tval(c, i, k)
                    return col(table, n)
                if 0 <= c + 1 < T:
                    v.wait_ge(s_xhi, tval(c, i, 2))
                    V.tensor_tensor(xt[:, (c + 1) % 2, LO, :, :], p_tx.rearrange("p (k n) -> p k n", k=KD),
                                    xt[:, (c + 1) % 2, HI, :, :], ALU.subtract).then_inc(s_xlo, 1)
                if 0 <= c + 2 < T:
                    n = tval(c, i, 3)
                    v.wait_ge(s_xld[c % 2], tval((c + 2) // 2, i, 1, 3) * 16)
                    row_max(small[:, 0:1], xrow[:, c % 2, :]).then_inc(s_xmx, 1)
                    v.wait_ge(s_xmx, n)
                    exponent(small[:, 1:2], small[:, 0:1]).then_inc(s_xex, 1)
                    v.wait_ge(s_xex, n)
                    inverse(tab(xinv, 2), small[:, 1:2]).then_inc(s_xiv, 1)
                    v.wait_ge(s_xiv, n)
                    if c + 2 >= 2:
                        v.wait_ge(s_xs, tval(c, i, 1))
                    scale_of(small[:, 2 + c % 2:3 + c % 2], tab(xinv, 2)).then_inc(s_xsc, 1)
                if 0 <= c - 3 < QN:
                    wmax(c - 3, i)
                if 0 <= c - 1 < T:
                    v.wait_ge(s_hhi, tval(c, i))
                    V.tensor_tensor(xt[:, c % 2, LO, :, :], p_th.rearrange("p (k n) -> p k n", k=KD),
                                    xt[:, c % 2, HI, :, :], ALU.subtract).then_inc(s_hlo, 1)
                if 0 <= c - 3 < QN:
                    wscale(c - 3, i)
                if 0 <= c < T:
                    n = tval(c, i, 1)
                    v.wait_ge(s_h, n)
                    row_max(small[:, 4:5], p_h[c % 2]).then_inc(s_hmx, 1)
                    v.wait_ge(s_hmx, n)
                    exponent(small[:, 5:6], small[:, 4:5]).then_inc(s_hex, 1)
                    v.wait_ge(s_hex, n)
                    inverse(small[:, 6:7], small[:, 5:6]).then_inc(s_hiv, 1)
                    v.wait_ge(s_hiv, n)
                    if c >= 1:
                        v.wait_ge(s_hs, tval(c, i))
                    scale_of(small[:, 7:8], small[:, 6:7]).then_inc(s_hsc, 1)
                    V.tensor_scalar(tab(ch, 0), small[:, 6:7], tab(xinv, 0), rexp[:, 1, 0:1],
                                    ALU.mult, ALU.mult).then_inc(s_ch, 1)
                if 0 <= c - 1 < T:
                    v.wait_ge(s_rt, tval(c, i))
                    v.wait_ge(s_ch, tval(c, i))
                    V.tensor_scalar(rlog[:, :, :].rearrange("p a e -> p (a e)"), p_rt, tab(ch, -1), rexp[:, 1, 2:3],
                                    ALU.mult, ALU.mult).then_inc(s_rlog, 1)
                    v.wait_ge(s_rlog, tval(c, i))
                    t1 = tval(c, i, -1)
                    dst = logits[:, t1, :] if i is None else logits[:, ds(t1, 1), :].rearrange("p a e -> p (a e)")
                    V.tensor_tensor(dst, rlog[:, 0, :], rlog[:, 1, :], ALU.add).then_inc(s_log, 1)
                if 0 <= c - 3 < QN:
                    wlow(c - 3, i)

            def wmax(c, i):
                kind, e = chunk(c, i)
                per6 = 16 * 4
                got = 16 * sum(2 if k % 3 == DOWN else 1 for k in range(c % 2, c + 1, 2))
                v.wait_ge(s_wld[c % 2], got if i is None else i * per6 + got)
                if kind == DOWN:
                    v.wait_ge(s_pad, tval(c // 3, i, 1, 2))
                _, src = w_views(c, i, LO)
                row_max(small[:, 12:13], src, mybir.AxisListType.XY).then_inc(s_wmx, 1)

            def wscale(c, i):
                kind, e = chunk(c, i)
                n = tval(c, i, 1)
                inv = winv[:, kind, e:e + 1] if isinstance(e, int) else winv[:, kind, ds(e, 1)]
                v.wait_ge(s_war, n)
                exponent(small[:, 14:15], small[:, 13:14]).then_inc(s_wex, 1)
                v.wait_ge(s_wex, n)
                inverse(inv, small[:, 14:15]).then_inc(s_wiv, 1)
                v.wait_ge(s_wiv, n)
                scale_of(small[:, 15:16], inv).then_inc(s_wsc, 1)

            def wlow(c, i):
                hi, src = w_views(c, i, HI)
                lo, _ = w_views(c, i, LO)
                v.wait_ge(s_whi, tval(c, i, 1))
                V.scalar_tensor_tensor(out=lo, in0=src, scalar=small[:, 15:16], in1=hi,
                                       op0=ALU.mult, op1=ALU.subtract).then_inc(s_wfree, 1)

            for c in range(-2, 3):
                step(c)
            with v.Fori(0, 4) as i:
                for c in range(3, 9):
                    step(c, i)
            for c in range(27, T + 1):
                step(c)

            chain = [0]

            def link(ins):
                chain[0] += 1
                ins.then_inc(s_r, 1)
                v.wait_ge(s_r, chain[0])

            def by_t(a_):
                return a_.unsqueeze(2).broadcast_to([P, T, E])

            def by_e(a_, n=T):
                return a_.unsqueeze(1).broadcast_to([P, n, E])

            v.wait_ge(s_log, T)
            v.wait_ge(s_hst, 16 * T)
            link(V.tensor_reduce(r_max, logits[:, :, :], AX, ALU.max))
            V.tensor_tensor(te(r_s), logits[:, :, :], by_t(r_max), ALU.subtract).then_inc(s_rd, 1)
            v.wait_ge(s_re, 1)
            link(V.tensor_reduce(r_sum, te(r_s), AX, ALU.add))
            link(V.reciprocal(r_sum, r_sum))
            link(V.tensor_tensor(te(r_s), te(r_s), by_t(r_sum), ALU.mult))

            def pick(scores, value, lowest, onehot):
                link(V.tensor_reduce(value, te(scores), AX, ALU.max))
                link(V.tensor_tensor(te(r_eq), te(scores), by_t(value), ALU.is_equal))
                link(V.scalar_tensor_tensor(out=te(r_cand), in0=te(r_eq), scalar=float(-E), in1=by_e(iota_e[:, :]),
                                            op0=ALU.mult, op1=ALU.add))
                link(V.tensor_reduce(lowest, te(r_cand), AX, ALU.min))
                link(V.tensor_tensor(te(onehot), te(r_cand), by_t(lowest), ALU.is_equal))

            pick(r_s, r_v1, r_e1, r_oh1)
            link(V.scalar_tensor_tensor(out=r_s2, in0=r_oh1, scalar=-2.0, in1=r_s, op0=ALU.mult, op1=ALU.add))
            pick(r_s2, r_v2, r_e2, r_oh2)
            V.tensor_tensor(m16, r_oh1, r_oh2, ALU.add).then_inc(s_m16, 1)
            v.wait_ge(s_const, 7)
            for k, val in ((0, r_v1), (1, r_v2)):
                link(V.tensor_copy(pay[:, :, k, 1], ch[:, :]))
                link(V.tensor_copy(pay[:, :, k, 2], val))
            v.wait_ge(s_rmm, 2)
            link(V.tensor_copy(r_cs, p_count))
            src, dst = r_cs, r_in0
            d_ = 1
            while d_ < T:
                link(V.tensor_tensor(dst[:, d_ * E:TE], src[:, d_ * E:TE], src[:, 0:TE - d_ * E], ALU.add))
                link(V.tensor_copy(dst[:, 0:d_ * E], src[:, 0:d_ * E]))
                src, dst = dst, (r_in1 if dst is r_in0 else r_in0)
                d_ *= 2
            link(V.tensor_scalar(r_n, src[:, TE - E:TE], float(P - 1), None, ALU.add))
            link(V.tensor_copy(r_tmp.bitcast(I32), r_n))
            link(V.tensor_scalar(r_tmp.bitcast(I32), r_tmp.bitcast(I32), P.bit_length() - 1, None,
                                 ALU.arith_shift_right))
            link(V.tensor_copy(r_tiles, r_tmp.bitcast(I32)))
            link(V.tensor_copy(r_end, r_tiles))
            for e in range(1, E):
                link(V.tensor_tensor(r_end[:, e:e + 1], r_end[:, e:e + 1], r_end[:, e - 1:e], ALU.add))
            link(V.tensor_tensor(r_base, r_end, r_tiles, ALU.subtract))
            link(V.tensor_scalar(r_base, r_base, float(P), None, ALU.mult))
            link(V.tensor_tensor(dst, src, r_cs, ALU.subtract))
            link(V.tensor_tensor(dst, dst, p_rank, ALU.add))
            link(V.tensor_tensor(te(dst), te(dst), by_e(r_base), ALU.add))
            for k, onehot in ((0, r_oh1), (1, r_oh2)):
                link(V.tensor_tensor(r_eq, onehot, dst, ALU.mult))
                link(V.tensor_reduce(r_e1, te(r_eq), AX, ALU.add))
                V.tensor_copy(pos[:, :, k], r_e1).then_inc(s_pay, 1)
                v.wait_ge(s_pay, k + 1)
            for half in range(2):
                for base, t0, t1 in ((0, 0, S1T), (ET, S1T, T)):
                    for table, kind in ((cg, GATE), (cu, UP), (cd, DOWN)):
                        sel = table[:, base + 2 * t0:base + 2 * t1].rearrange("p (t s) -> p t s", s=2)[:, :, half]
                        w_ = winv[:, kind, E + half:E + half + 1]
                        if kind == DOWN:
                            V.tensor_copy(sel, w_.broadcast_to([P, t1 - t0])).then_inc(s_coef, 1)
                        else:
                            V.tensor_scalar(sel, ch[:, t0:t1], w_, None, ALU.mult).then_inc(s_coef, 1)
            v.wait_ge(s_coef, 12)
            ej = [P, ET, E]
            link(V.tensor_tensor(j_a, iota_j[:, :].unsqueeze(2).broadcast_to(ej), r_end.unsqueeze(1).broadcast_to(ej),
                                 ALU.is_ge))
            link(V.tensor_reduce(cy[:, 0:ET], j_a, AX, ALU.add))
            link(V.tensor_scalar(cy[:, 0:ET], cy[:, 0:ET], float(E - 1), None, ALU.min))
            V.tensor_copy(etile[:, :], cy[:, 0:ET]).then_inc(s_et, 1)
            link(V.tensor_tensor(j_a, iota_e[:, :].unsqueeze(1).broadcast_to(ej), cy[:, 0:ET].unsqueeze(2).broadcast_to(ej),
                                 ALU.is_equal))
            for table, kind in ((cg, GATE), (cu, UP), (cd, DOWN)):
                link(V.tensor_tensor(j_b, j_a, winv[:, kind, 0:E].unsqueeze(1).broadcast_to(ej), ALU.mult))
                link(V.tensor_reduce(table[:, N1:N2], j_b, AX, ALU.add))

            def slot(s, prev):
                if s and s.last and s.c < NS - 1:
                    v.wait_ge(s_fhi, s.h + 2)
                    V.tensor_tensor(ht[:, 1 - s.hpar, LO, :, :], p_fth.rearrange("p (k n) -> p k n", k=KD),
                                    ht[:, 1 - s.hpar, HI, :, :], ALU.subtract).then_inc(s_flo, 1)
                if prev:
                    v.wait_ge(s_ahi, prev.n + 1)
                    V.tensor_tensor(at[:, prev.par, LO, :, :].rearrange("p k n -> p (k n)"), p_at[:, 0:KH * P],
                                    at[:, prev.par, HI, :, :].rearrange("p k n -> p (k n)"),
                                    ALU.subtract).then_inc(s_alo, 1)
                if s and s.c == N1:
                    v.wait_ge(s_metain, 16)
                    for table, k in ((cg, 1), (cu, 1), (cd, 2)):
                        V.tensor_tensor(table[:, N1:N2], table[:, N1:N2], meta[:, :, k], ALU.mult).then_inc(s_coef, 1)
                    v.wait_ge(s_coef, 15)
                if s:
                    n = s.n + 1
                    v.wait_ge(s_silu, n)
                    V.scalar_tensor_tensor(out=act[:, :], in0=p_u[s.par], scalar=col(cu, s.n), in1=act[:, :],
                                           op0=ALU.mult, op1=ALU.mult).then_inc(s_a, 1)
                    v.wait_ge(s_a, n)
                    row_max(fsm[:, 0:1], act[:, :]).then_inc(s_amx, 1)
                    v.wait_ge(s_amx, n)
                    exponent(fsm[:, 0:1], fsm[:, 0:1]).then_inc(s_aex, 1)
                    v.wait_ge(s_aex, n)
                    inverse(fsm[:, 1:2], fsm[:, 0:1]).then_inc(s_aiv, 1)
                    v.wait_ge(s_aiv, n)
                    scale_of(fsm[:, 2:3], fsm[:, 1:2]).then_inc(s_asc, 1)
                    V.tensor_tensor(col(cy, s.n), fsm[:, 1:2], col(cd, s.n), ALU.mult).then_inc(s_cy, 1)
                if prev and prev.shared:
                    v.wait_ge(s_dn, prev.n + 1)
                    v.wait_ge(s_cy, prev.n + 1)
                    if prev.half == 0:
                        v.wait_ge(s_xin[prev.tpar], 16 * (prev.tq + 1))
                    else:
                        v.wait_ge(s_acc, prev.k)
                    V.scalar_tensor_tensor(out=acc[:, prev.tpar, :], in0=p_y[prev.par], scalar=col(cy, prev.n),
                                           in1=acc[:, prev.tpar, :], op0=ALU.mult, op1=ALU.add).then_inc(s_acc, 1)

            v.wait_ge(s_fhi, 1)
            V.tensor_tensor(ht[:, 0, LO, :, :], p_fth.rearrange("p (k n) -> p k n", k=KD),
                            ht[:, 0, HI, :, :], ALU.subtract).then_inc(s_flo, 1)
            run_slots(v, slot)
            tail(slot)

        @block.tensor
        def _(pe):
            w_src = stage[:, :, :].rearrange("p b n -> p (b n)")
            pe.wait_ge(s_pin, 16 * (2 + NA + 2 + NA))
            pe.wait_ge(s_const, 1)
            for k in range(KD):
                for c in range(KD):
                    mm = pe.transpose(ps[:, k, c * P:(c + 1) * P], w_src[:, c * D + k * P:c * D + (k + 1) * P],
                                      ident[:, :])
                mm.then_inc(s_pt, 1)
            for j in range(2):
                for c in range(KD):
                    o = KD * D + j * D + c * P
                    mm = pe.transpose(ps[:, KD + j, c * P:(c + 1) * P], w_src[:, o:o + P], ident[:, :])
                mm.then_inc(s_pt, 1)
            pe.wait_ge(s_pt, KD + 2)
            pe.sem_inc(s_wfree, 2)

            def split_matmul(dst, lhs, rhs, n, stop):
                parts = [(k, a_, b_) for k in range(n) for a_, b_ in ((HI, HI), (HI, LO), (LO, HI))]
                for m, (k, a_, b_) in enumerate(parts):
                    mm = pe.matmul(dst, lhs(k, a_), rhs(k, b_), start=(m == 0), stop=(stop and m == len(parts) - 1))
                return mm

            def step(c, i=None):
                b = c % 2
                if 0 <= c + 1 < T:
                    pe.wait_ge(s_xs, tval(c, i, 2))
                    if c >= 0:
                        pe.wait_ge(s_xlo, tval(c, i, 1))
                    else:
                        pe.wait_ge(s_phi, KD + 3)
                        pe.wait_ge(s_plo, KD + 3)
                    for k in range(KD):
                        mm = pe.transpose(p_tx[:, k * P:(k + 1) * P], xrow[:, 1 - b, k * P:(k + 1) * P], ident[:, :])
                    mm.then_inc(s_tx, 1)
                if 0 <= c < T:
                    pe.wait_ge(s_xlo, tval(c, i, 1))
                    if c >= 1:
                        pe.wait_ge(s_xam, tval(c, i))
                    split_matmul(p_xa, lambda k, a_: lat[:, k, a_, :], lambda k, b_: xt[:, b, b_, k, :],
                                 KD, True).then_inc(s_xa, 1)
                    if c >= 2:
                        pe.wait_ge(s_hs, tval(c, i, -1))
                    split_matmul(p_h[b], lambda k, a_: xt[:, b, a_, k, :], lambda k, b_: cw[:, k, b_, :], KD, False)
                if 0 <= c - 1 < T:
                    pe.wait_ge(s_hs, tval(c, i))
                    if c >= 2:
                        pe.wait_ge(s_hlo, tval(c, i, -1))
                    for k in range(KD):
                        mm = pe.transpose(p_th[:, k * P:(k + 1) * P], hs[:, k * P:(k + 1) * P], ident[:, :])
                    mm.then_inc(s_th, 1)
                if 0 <= c < T:
                    pe.wait_ge(s_xam, tval(c, i, 1))
                    pe.matmul(p_h[b], xam[:, :], lbt[:, :], start=False, stop=True).then_inc(s_h, 1)
                if 0 <= c - 1 < T:
                    pe.wait_ge(s_hlo, tval(c, i))
                    if c >= 2:
                        pe.wait_ge(s_log, tval(c, i, -1))
                    for k in range(KD):
                        for a_ in (HI, LO):
                            mm = pe.matmul(p_rt, xt[:, b, a_, k, :], wr[:, k, :, :].rearrange("p a e -> p (a e)"),
                                           start=(k == 0 and a_ == HI), stop=(k == KD - 1 and a_ == LO))
                    mm.then_inc(s_rt, 1)

            for c in range(-2, 3):
                step(c)
            with pe.Fori(0, 4) as i:
                for c in range(3, 9):
                    step(c, i)
            for c in range(27, T + 1):
                step(c)

            pe.wait_ge(s_m16, 1)
            pe.wait_ge(s_const, 7)
            pe.matmul(p_rank, upper16, m16, start=True, stop=True).then_inc(s_rmm, 1)
            pe.matmul(p_count, ones16, m16, start=True, stop=True).then_inc(s_rmm, 1)

            def transpose_rows(hc, i):
                hpar = hc % 2
                if hc < H1:
                    landed, count = s_hin, hc // 2 + 1
                elif hc < H2:
                    landed, count = s_hgat, (hc - H1) // 2 + 1
                else:
                    landed, count = s_hin, (H1 + 1 - hpar) // 2 + (hc - H2) // 2 + 1
                pe.wait_ge(landed[hpar], tval(count, i, 0, 1) * 16)
                for k in range(KD):
                    mm = pe.transpose(p_fth[:, k * P:(k + 1) * P], hin[:, hpar, k * P:(k + 1) * P], ident[:, :])
                mm.then_inc(s_fth, 1)

            def weights(w, s, e, k, half):
                if s.shared:
                    return w[:, s.expert, k, half, :]
                return w[:, ds(e, 1), k, half, :].rearrange("p a n -> p (a n)")

            def expert_of(s):
                if s.shared:
                    return None
                o = etile[0:1, s.j:s.j + 1] if isinstance(s.j, int) else etile[0:1, ds(s.j, 1)]
                return pe.value_load(o, min_val=0, max_val=E - 1)

            def slot(s, prev):
                if s:
                    if s.c == N1:
                        pe.wait_ge(s_et, 1)
                    e = expert_of(s)
                    if s.last and s.c < NS - 1:
                        pe.wait_ge(s_flo, s.h + 1)
                        transpose_rows(s.hc + 1, s.i)
                    pe.wait_ge(s_flo, s.h + 1)
                    if s.c >= 2:
                        pe.wait_ge(s_silu, s.n - 1)
                        pe.wait_ge(s_a, s.n - 1)
                    for k in range(KD):
                        for wh in (HI, LO):
                            for w, dst in ((wg, p_g), (wu, p_u)):
                                pe.matmul(dst[s.par], ht[:, s.hpar, HI, k, :], weights(w, s, e, k, wh),
                                          start=(k == 0 and wh == HI), stop=False)
                if prev:
                    pe.wait_ge(s_as, prev.n + 1)
                    if prev.c >= 1:
                        pe.wait_ge(s_alo, prev.n)
                    for k in range(KH):
                        m = P if k < KH - 1 else HR
                        mm = pe.transpose(p_at[0:m, k * P:(k + 1) * P], act[:, k * P:k * P + m], ident[:, :])
                    mm.then_inc(s_ta, 1)
                if s:
                    for k in range(KD):
                        for w, dst in ((wg, p_g), (wu, p_u)):
                            mm = pe.matmul(dst[s.par], ht[:, s.hpar, LO, k, :], weights(w, s, e, k, HI),
                                           start=False, stop=(k == KD - 1))
                    mm.then_inc(s_gu, 1)
                if prev:
                    e = expert_of(prev)
                    pe.wait_ge(s_alo, prev.n + 1)
                    if 2 <= prev.c < N1 + 2:
                        pe.wait_ge(s_acc, prev.n - 1)
                    elif N1 + 2 <= prev.c < N2 + 2:
                        pe.wait_ge(s_y, prev.n - 1 - N1)
                    elif prev.c >= N2 + 2:
                        pe.wait_ge(s_acc, prev.n - 1 - ET)
                    parts = [(k, a_, b_) for k in range(KH) for a_, b_ in ((HI, HI), (HI, LO), (LO, HI))]
                    for m, (k, a_, b_) in enumerate(parts):
                        rows = P if k < KH - 1 else HR
                        mm = pe.matmul(p_y[prev.par], at[0:rows, prev.par, a_, k, :], weights(wd, prev, e, k, b_)[0:rows],
                                       start=(m == 0), stop=(m == len(parts) - 1))
                    mm.then_inc(s_dn, 1)

            pe.wait_ge(s_log, T)
            pe.wait_ge(s_hs, T)
            transpose_rows(0, None)
            run_slots(pe, slot)
            tail(slot)


_INS = ['x', 'itok_B_0_6', 'L0_cond_W', 'L0_cond_A', 'L0_cond_Bm', 'L0_cond_scalings', 'L0_ffn_W_router',
        'L0_ffn_We_gate', 'L0_ffn_We_up', 'L0_ffn_We_down', 'L0_ffn_Ws_gate', 'L0_ffn_Ws_up', 'L0_ffn_Ws_down']
_OUTS = [((16, 256, 512), 'float32')]


def kernel(**inputs):
    import numpy as _np
    import concourse.bacc as _bacc
    from concourse import mybir as _mybir
    from concourse.bass_utils import run_bass_kernel_spmd as _run

    nc = _bacc.Bacc("TRN2", target_bir_lowering=False, num_devices=1)
    arrays, args = {}, []
    for name in _INS:
        a = _np.ascontiguousarray(inputs[name])
        arrays[f"in_{name}_dram"] = a
        args.append(nc.dram_tensor(f"in_{name}_dram", a.shape, _mybir.dt.from_np(a.dtype), kind="ExternalInput").ap())
    for i, (shape, dtype) in enumerate(_OUTS):
        dt = _mybir.dt.from_np(_np.dtype(dtype))
        args.append(nc.dram_tensor(f"out_{i}_dram", shape, dt, kind="ExternalOutput").ap())
    adaln_moe_kernel(nc, *args)
    r = _run(nc, [arrays], core_ids=[0])
    got = tuple(r.results[0][f"out_{i}_dram"] for i in range(len(_OUTS)))
    return got[0]
```

```python
from contextlib import ExitStack

import concourse.bass as bass
from concourse import mybir

F32, F16, I32 = mybir.dt.float32, mybir.dt.float16, mybir.dt.int32
ALU = mybir.AluOpType
ACT = mybir.ActivationFunctionType
AX = mybir.AxisListType.X

P = 128
HI, LO = 0, 1
GATE, UP, DOWN = 0, 1, 2

EXP_MASK = 0x7F800000
ONE_EXP = 1 << 23
TOP = 14
MIN_EXP = 27


def adaln_moe_kernel(nc, x, adapter_idx, cond_w, lora_a, lora_b, scalings, w_router,
                     we_gate, we_up, we_down, ws_gate, ws_up, ws_down, out):
    B, S, D = x.shape
    NA, RANK, _ = lora_a.shape
    E, _, H = we_gate.shape
    assert NA * RANK == P and ws_gate.shape[1] == 2 * H and D == 4 * P
    TOKENS = B * S
    T = TOKENS // P
    TPB = S // P
    KD = D // P
    KH = -(-H // P)
    HR = H - (KH - 1) * P
    EX = E + 2
    ET = 2 * TOKENS // P + E - 1
    S1T = 11
    LEAD = 6
    N1 = 2 * S1T
    N2 = N1 + ET
    NS = N2 + 2 * (T - S1T)
    H1 = S1T
    H2 = H1 + ET
    SLOTS = (ET + 1) * P
    assert TPB == 2 and ET % 2 == 1 and S1T % 2 == 1 and (T - S1T) % 2 == 1 and N1 % 2 == 0

    x_rows = x.rearrange("b (t p) d -> (b t) p d", p=P)
    out_rows = out.rearrange("b (t p) d -> (b t) p d", p=P)
    h_dram = nc.dram_tensor("h_dram", [TOKENS, 2 * D], F16).ap()
    y_dram = nc.dram_tensor("y_dram", [ET * P, D], F32).ap()
    part_dram = nc.dram_tensor("part_dram", [S1T * P, D], F32).ap()
    meta_dram = nc.dram_tensor("meta_dram", [SLOTS, 4], F32).ap()
    h_tiles = h_dram.rearrange("(t p) d -> t p d", p=P)
    y_tiles = y_dram.rearrange("(t p) d -> t p d", p=P)
    part_tiles = part_dram.rearrange("(t p) d -> t p d", p=P)
    ds = bass.ds

    with ExitStack() as ctx:
        def sb(name, shape, dt, c=ctx):
            return c.enter_context(nc.sbuf_tensor(name, shape, dt))

        def sem(name):
            return ctx.enter_context(nc.semaphore(name))

        wg = sb("wg", [P, EX, KD, 2, H], F16)
        wu = sb("wu", [P, EX, KD, 2, H], F16)
        wd = sb("wd", [P, EX, KH, 2, D], F16)
        ident16 = sb("ident16", [P, P], F16)
        ch = sb("ch", [P, T], F32)
        winv = sb("winv", [P, 3, EX], F32)
        iota_e = sb("iota_e", [P, E], F32)
        scale_c = sb("scale_c", [P, 2], F32)
        iota_j = sb("iota_j", [P, ET], F32)

        actx = ExitStack()
        stage = sb("stage", [P, 2, KH * D], F32, actx)
        cw = sb("cw", [P, KD, 2, D], F16, actx)
        lat = sb("lat", [P, KD, 2, P], F16, actx)
        lbt = sb("lbt", [P, D], F32, actx)
        wr = sb("wr", [P, KD, 2, E], F16, actx)
        lmask = sb("lmask", [P, B], F32, actx)
        xrow = sb("xrow", [P, 2, D], F32, actx)
        x16 = sb("x16", [P, 2, D], F16, actx)
        xt = sb("xt", [P, 2, 2, KD, P], F16, actx)
        xam = sb("xam", [P, P], F32, actx)
        xinv = sb("xinv", [P, T], F32, actx)
        small = sb("small", [P, 16], F32, actx)
        rlog = sb("rlog", [P, 2, E], F32, actx)
        rexp = sb("rexp", [P, 3, 4], F32, actx)
        h16 = sb("h16", [P, 2, D], F16, actx)
        early = h16[:, :, :].rearrange("p a d -> p (a d)").bitcast(F32)
        ident = early[:, 0:P]
        wr32 = early[:, P:P + KD * E].rearrange("p (k e) -> p k e", k=KD)
        pcol = early[:, P + KD * E:P + KD * E + 4]
        actx.close()
        stage_down = wd[:, E, :, :, :].rearrange("p k a d -> p (k a d)").bitcast(F32)

        route = sb("route", [P, 3072], F32)
        hin = sb("hin", [P, 2, 2, D], F16)
        ht = sb("ht", [P, 2, 2, KD, P], F16)
        cg = sb("cg", [P, NS], F32)
        cu = sb("cu", [P, NS], F32)
        cd = sb("cd", [P, NS], F32)
        cy = sb("cy", [P, NS], F32)
        fsm = sb("fsm", [P, 4], F32)
        idx = sb("idx", [P, 2], I32)
        posb = sb("posb", [P, 6], I32)
        act = sb("act", [P, H], F32)
        a16 = sb("a16", [P, 2, H], F16)
        at = sb("at", [P, 2, 2, KH, P], F16)
        acc = sb("acc", [P, 2, D], F32)
        meta = sb("meta", [P, ET, 4], F32)
        pos = sb("pos", [P, T, 2], I32)
        etile = sb("etile", [P, ET], I32)
        part = sb("part", [P, D], F32)
        yout = route[:, 0:2 * D].rearrange("p (b d) -> p b d", b=2)
        gat = route[:, 2 * D:6 * D].rearrange("p (b s d) -> p b s d", b=2, s=2)

        at_ = [0]

        def take(n):
            at_[0] += n
            return route[:, at_[0] - n:at_[0]]

        def te(v):
            return v.rearrange("p (t e) -> p t e", e=E)

        TE = T * E
        r_s, r_eq, r_cand = take(TE), take(TE), take(TE)
        r_oh1, r_oh2 = take(TE), take(TE)
        r_s2, r_cs, r_in0, r_in1 = take(TE), take(TE), take(TE), take(TE)
        pay = take(TE).rearrange("p (t s c) -> p t s c", s=2, c=4)
        m16 = take(TE // 2).bitcast(F16)
        upper16, ones16 = take(P // 2).bitcast(F16), take(P // 2).bitcast(F16)
        r_max, r_sum, r_v1, r_e1, r_v2, r_e2 = [take(T) for _ in range(6)]
        r_n, r_tiles, r_end, r_base, r_tmp = [take(E) for _ in range(5)]
        assert at_[0] <= 3072 and ET * E <= 3 * TE
        j_a = route[:, 0:ET * E].rearrange("p (j e) -> p j e", e=E)
        j_b = route[:, 5 * TE:5 * TE + ET * E].rearrange("p (j e) -> p j e", e=E)

        ps = ctx.enter_context(nc.psum_tensor("ps", [P, 8, 512], F32))
        def halves(bank, k):
            return ps[:, bank, 0:k * P].bitcast(F16).rearrange("p (a k n) -> p a k n", a=2, k=k)
        p_tx, p_th, p_xa, p_rt = halves(0, KD), halves(1, KD), ps[:, 2, 0:P], ps[:, 3, 0:2 * E]
        p_h = [ps[:, 4, :], ps[:, 5, :]]
        p_rank, p_count = ps[:, 0, 0:TE], ps[:, 0, TE:2 * TE]
        logits = ps[:, 7, 0:T * E].rearrange("p (t e) -> p t e", e=E)
        p_fth, p_at = halves(0, KD), halves(1, KH)
        p_g = [ps[:, 2, 0:H], ps[:, 3, 0:H]]
        p_u = [ps[:, 4, 0:H], ps[:, 5, 0:H]]
        p_y = [ps[:, 6, :], ps[:, 7, :]]

        s_const = sem("s_const")
        s_cw, s_la, s_pin = sem("s_cw"), sem("s_la"), sem("s_pin")
        s_csum, s_pmx = sem("s_csum"), sem("s_pmx")
        s_par = sem("s_par")
        s_pc = sem("s_pc")
        s_pt = sem("s_pt")
        s_phi = sem("s_phi")
        s_plo = sem("s_plo")
        s_z = sem("s_z")
        s_meta0 = sem("s_meta0")
        s_xld = [sem("s_xld0"), sem("s_xld1")]
        s_xmx, s_xex, s_xiv, s_xsc = sem("s_xmx"), sem("s_xex"), sem("s_xiv"), sem("s_xsc")
        s_xhi, s_xlo, s_tx, s_xt = sem("s_xhi"), sem("s_xlo"), sem("s_tx"), sem("s_xt")
        s_xa, s_xam, s_h = sem("s_xa"), sem("s_xam"), sem("s_h")
        s_hmx, s_hex, s_hiv, s_hsc = sem("s_hmx"), sem("s_hex"), sem("s_hiv"), sem("s_hsc")
        s_ch, s_hst = sem("s_ch"), sem("s_hst")
        s_hhi, s_hlo, s_th, s_ht = sem("s_hhi"), sem("s_hlo"), sem("s_th"), sem("s_ht")
        s_rt, s_rlog, s_log = sem("s_rt"), sem("s_rlog"), sem("s_log")
        s_wld = [sem("s_wld_gate"), sem("s_wld_up"), sem("s_wld_down")]
        s_pad, s_wsum, s_war = sem("s_pad"), sem("s_wsum"), sem("s_war")
        s_wex, s_wiv, s_wsc, s_whi, s_wss, s_wfree = sem("s_wex"), sem("s_wiv"), sem("s_wsc"), sem("s_whi"), sem("s_wss"), sem("s_wfree")
        s_r = sem("s_r")
        s_rd, s_re, s_m16, s_rmm, s_rcp = sem("s_rd"), sem("s_re"), sem("s_m16"), sem("s_rmm"), sem("s_rcp")
        s_pay, s_scat, s_metain, s_et = sem("s_pay"), sem("s_scat"), sem("s_metain"), sem("s_et")
        s_coef = sem("s_coef")
        s_hin = [sem("s_hin0"), sem("s_hin1")]
        s_hgat = [sem("s_hgat0"), sem("s_hgat1")]
        s_fth, s_fht = sem("s_fth"), sem("s_fht")
        s_gu, s_silu, s_a = sem("s_gu"), sem("s_silu"), sem("s_a")
        s_amx, s_aex, s_aiv, s_asc, s_cy = (sem("s_amx"), sem("s_aex"), sem("s_aiv"), sem("s_asc"),
                                            sem("s_cy"))
        s_ahi, s_alo, s_ta, s_at, s_dn = sem("s_ahi"), sem("s_alo"), sem("s_ta"), sem("s_at"), sem("s_dn")
        s_y = sem("s_y")
        s_yst = [sem("s_yst0"), sem("s_yst1")]
        s_xin = [sem("s_xin0"), sem("s_xin1")]
        s_acc = sem("s_acc")
        s_pst = [sem("s_pst0"), sem("s_pst1")]
        s_ix = sem("s_ix")
        s_g = [sem("s_g0"), sem("s_g1")]
        s_pld, s_ge, s_oute = sem("s_pld"), sem("s_ge"), sem("s_oute")
        s_ixl, s_ixe, s_addl, s_adde = sem("s_ixl"), sem("s_ixe"), sem("s_addl"), sem("s_adde")
        s_out = [sem("s_out0"), sem("s_out1")]

        block = ctx.enter_context(nc.Block())

        def tval(c, i, k=0, per=6):
            return c + k if i is None else c + k + i * per

        def chunk(c, i):
            if c < 3:
                return c % 3, E + 1
            return c % 3, tval(c // 3 - 1, i, 0, 2)

        QN = 3 * EX

        class Slot:
            def __init__(s, c, i=None):
                shared = c < N1 or c >= N2
                per = 4 if shared else 2
                s.i = i
                s.c, s.n, s.par = c, tval(c, i, 0, per), c % 2
                s.shared = shared
                if shared:
                    m = c if c < N1 else c - N2
                    tile = m // 2 if c < N1 else S1T + m // 2
                    s.half = m % 2
                    s.hc = m // 2 if c < N1 else H2 + m // 2
                    s.h, s.tile, s.tpar = tval(s.hc, i, 0, 2), tval(tile, i, 0, 2), tile % 2
                    s.tq = tval(tile // 2, i, 0, 1)
                    s.first = c < N1
                    s.expert = E + s.half
                    s.last = s.half == 1
                    s.k = tval(m if c < N1 else c - ET, i, 0, 4)
                else:
                    s.hc = H1 + c - N1
                    s.h, s.j, s.last = tval(s.hc, i, 0, 2), tval(c - N1, i, 0, 2), True
                s.hpar = s.hc % 2

        def run_slots(eng, do, after=None):
            def straight(c):
                do(Slot(c), Slot(c - 1) if c else None)
                if after and c < LEAD:
                    after(c)

            def loop(start, count, per):
                with eng.Fori(0, count) as i:
                    for c in range(start, start + per):
                        prev = Slot(c - 1, i)
                        do(Slot(c, i), prev)
            for start, end, per, lead in ((0, N1, 4, LEAD), (N1, N2, 2, 3), (N2, NS, 4, 3)):
                for c in range(start, start + lead):
                    straight(c)
                count = (end - start - lead - 1) // per
                loop(start + lead, count, per)
                for c in range(start + lead + count * per, end):
                    straight(c)

        def tail(do):
            do(None, Slot(NS - 1))

        def yst_before(s):
            return (s.c - N1) // 2 * 16 if isinstance(s.j, int) else (s.j - (s.c - N1)) * 8 + (s.c - N1) // 2 * 16

        def col(table, n):
            return table[:, n:n + 1] if isinstance(n, int) else table[:, ds(n, 1)]

        def landing(c):
            return stage_down if c % 3 == DOWN and c != QN - 1 else stage[:, c % 3 % 2, :]

        def landed(c, i):
            if c == QN - 1:
                return s_wld[GATE], 16 * EX + 32
            return s_wld[c % 3], tval(c // 3, i, 1, 2) * (32 if c % 3 == DOWN else 16)

        def w_views(c, i, half):
            kind, e = chunk(c, i)
            w = (wg, wu, wd)[kind]
            k, n = (KH, D) if kind == DOWN else (KD, H)
            dst = w[:, e, :, half, :] if isinstance(e, int) else \
                w[:, ds(e, 1), :, half, :].rearrange("p a k n -> p (a k) n")
            return dst, landing(c)[:, 0:k * n].rearrange("p (k n) -> p k n", k=k)

        @block.sync
        def _(sp):
            def load_x(c, i):
                t = tval(c, i)
                if c >= 2:
                    sp.wait_ge(s_xlo, tval(c, i, -1))
                src = x_rows[t] if i is None else x_rows[ds(t, 1)].rearrange("a p d -> (a p) d")
                sp.dma_start(xrow[:, c % 2, :], src).then_inc(s_xld[c % 2], 16)

            w_src = stage[:, :, :].rearrange("p b n -> p (b n)")
            sp.dma_start(w_src[:, KD * D:KD * D + D], lora_a.rearrange("a r d -> (a r) d")).then_inc(s_la, 16)
            sp.dma_start(w_src[:, 0:KD * D].rearrange("p (c d) -> p c d", c=KD),
                         cond_w.rearrange("(c p) d -> p c d", p=P)).then_inc(s_cw, 16)
            sp.dma_start(wr32, w_router.rearrange("(k p) e -> p k e", p=P)).then_inc(s_la, 16)
            load_x(0, None)
            sp.dma_start(pcol[:, 0:1], scalings.unsqueeze(1).broadcast_to([NA, RANK])).then_inc(s_pin, 16)
            sp.dma_start(lmask[:, :].bitcast(I32), adapter_idx.partition_broadcast(P)).then_inc(s_pin, 16)
            for c in range(KD):
                sp.dma_start(
                    w_src[:, KD * D + D + c * P:KD * D + D + (c + 1) * P].rearrange("p (a r) -> p a r", a=NA),
                    lora_b[:, c * P:(c + 1) * P, :].rearrange("a p r -> p a r")).then_inc(s_pin, 16)
            load_x(1, None)

            def load_w(c, i):
                kind, e = chunk(c, i)
                if c == 0:
                    sp.wait_ge(s_pmx, 2)
                    sp.wait_ge(s_csum, 1)
                    sp.wait_ge(s_pt, KD + 2)
                elif c == QN - 1:
                    sp.wait_ge(s_wfree, QN - 2)
                elif c >= 3:
                    sp.wait_ge(s_wfree, tval(c, i, -2))
                if i is None and e >= E:
                    half = e - E
                    src = [ws_gate[:, half * H:(half + 1) * H], ws_up[:, half * H:(half + 1) * H],
                           ws_down[half * H:(half + 1) * H, :]][kind]
                else:
                    src = [we_gate, we_up, we_down][kind]
                    src = src[e] if i is None else src[ds(e, 1)].rearrange("a r n -> (a r) n")
                dst, signal = landing(c), landed(c, i)[0]
                if kind == DOWN:
                    whole = (KH - 1) * P
                    sp.dma_start(dst[:, 0:(KH - 1) * D].rearrange("p (k d) -> p k d", d=D),
                                 src[0:whole, :].rearrange("(k p) d -> p k d", p=P)).then_inc(signal, 16)
                    sp.dma_start(dst[0:HR, (KH - 1) * D:KH * D], src[whole:H, :]).then_inc(signal, 16)
                else:
                    sp.dma_start(dst[:, 0:KD * H].rearrange("p (k h) -> p k h", h=H),
                                 src.rearrange("(k p) h -> p k h", p=P)).then_inc(signal, 16)

            def store_h(c, i):
                t = tval(c, i)
                sp.wait_ge(s_hlo, tval(c, i, 1))
                dst = h_tiles[t] if i is None else h_tiles[ds(t, 1)].rearrange("a p d -> (a p) d")
                sp.dma_start(dst, h16[:, :, :].rearrange("p a d -> p (a d)")).then_inc(s_hst, 16)

            def step(c, i=None):
                if 2 <= c + 3 < T:
                    load_x(c + 3, i)
                if 0 <= c - 1 < T:
                    store_h(c - 1, i)
                if 0 <= c + 1 < QN:
                    load_w(c + 1, i)

            for c in range(-1, 2):
                step(c)
            with sp.Fori(0, 4) as i:
                for c in range(2, 8):
                    step(c, i)
            for c in range(26, T + 1):
                step(c)

            sp.wait_ge(s_h, T)
            sp.wait_ge(s_hst, 16 * 2)

            def load_h(s):
                if s.c >= 2 * 2 or not s.first:
                    sp.wait_ge(s_fth, s.h - 1)
                src = h_tiles[s.tile] if isinstance(s.tile, int) else h_tiles[ds(s.tile, 1)].rearrange("a p d -> (a p) d")
                sp.dma_start(hin[:, s.hpar, :, :].rearrange("p a d -> p (a d)"), src).then_inc(s_hin[s.hpar], 16)

            def load_acc(s):
                if s.first and s.c >= 4:
                    sp.wait_ge(s_pst[s.tpar], s.tq * 16)
                elif not s.first:
                    if s.c < N2 + 4:
                        sp.wait_ge(s_pst[s.tpar], s.tq * 16)
                    else:
                        sp.wait_ge(s_out[s.tpar], (s.tq - S1T // 2 - (s.tpar == 0)) * 16)
                src = x_rows[s.tile] if isinstance(s.tile, int) else x_rows[ds(s.tile, 1)].rearrange("a p d -> (a p) d")
                sp.dma_start(acc[:, s.tpar, :], src).then_inc(s_xin[s.tpar], 16)

            def store_part(s):
                sp.wait_ge(s_acc, s.k + 1)
                dst = part_tiles[s.tile] if isinstance(s.tile, int) else part_tiles[ds(s.tile, 1)].rearrange("a p d -> (a p) d")
                sp.dma_start(dst, acc[:, s.tpar, :]).then_inc(s_pst[s.tpar], 16)

            def store_y(s):
                sp.wait_ge(s_y, s.j + 1)
                dst = y_tiles[s.j] if isinstance(s.j, int) else y_tiles[ds(s.j, 1)].rearrange("a p d -> (a p) d")
                sp.dma_start(dst, yout[:, s.par, :]).then_inc(s_yst[s.par], 16)

            for t in range(2):
                load_h(Slot(2 * t))
            sp.wait_ge(s_rt, T)
            for t in range(2):
                load_acc(Slot(2 * t))
            load_h(Slot(4))
            store_part(Slot(1))
            load_acc(Slot(4))
            with sp.Fori(0, (S1T - 3) // 2) as i:
                for t in range(1, 3):
                    load_h(Slot(2 * t + 4, i))
                    store_part(Slot(2 * t + 1, i))
                    load_acc(Slot(2 * t + 4, i))
            for t in range(S1T - 2, S1T):
                store_part(Slot(2 * t + 1))
            with sp.Fori(0, (ET - 3) // 2) as i:
                for c in range(N1, N1 + 2):
                    store_y(Slot(c, i))
            load_h(Slot(N2))
            load_acc(Slot(N2))
            store_y(Slot(N2 - 3))
            load_h(Slot(N2 + 2))
            load_acc(Slot(N2 + 2))
            store_y(Slot(N2 - 2))
            store_y(Slot(N2 - 1))
            load_h(Slot(N2 + 4))
            with sp.Fori(0, (T - S1T - 3) // 2) as i:
                for c in (N2 + 6, N2 + 8):
                    load_h(Slot(c, i))
                    load_acc(Slot(c - 2, i))
            load_acc(Slot(NS - 2))

        @block.gpsimd
        def _(pool):
            pool.memset(ident, 0.0).then_inc(s_z, 1)
            pool.wait_ge(s_z, 1)
            pool.affine_select(out=ident, in_=ident, compare_op=ALU.not_equal, fill=1.0, base=0,
                               pattern=[[-1, P]], channel_multiplier=1).then_inc(s_const, 1)
            pool.memset(scale_c[:, 0:1], float((254 + TOP) * ONE_EXP)).then_inc(s_const, 1)
            pool.memset(scale_c[:, 1:2], float((254 + TOP - MIN_EXP) * ONE_EXP)).then_inc(s_const, 1)
            pool.wait_ge(s_const, 3)
            pool.tensor_copy(ident16[:, :], ident).then_inc(s_const, 1)
            pool.iota(iota_e[:, :], [[1, E]], base=0, channel_multiplier=0,
                      allow_small_or_imprecise_dtypes=True).then_inc(s_const, 1)
            pool.iota(iota_j[:, :], [[1, ET]], base=0, channel_multiplier=0,
                      allow_small_or_imprecise_dtypes=True).then_inc(s_const, 1)
            pool.iota(pcol[:, 1:2].bitcast(I32), [[0, 1]], base=0, channel_multiplier=1).then_inc(s_const, 1)
            zeros = x16[:, :, :].rearrange("p a d -> p (a d)").bitcast(F32)[:, 0:SLOTS * 4 // P]
            pool.memset(zeros, 0.0).then_inc(s_z, 1)
            pool.wait_ge(s_z, 2)
            pool.dma_start(meta_dram.rearrange("(p j) c -> p (j c)", p=P), zeros).then_inc(s_meta0, 16)
            pool.memset(stage_down[HR:P, (KH - 1) * D:KH * D], 0.0).then_inc(s_pad, 1)
            pool.wait_ge(s_pad, 1)
            pool.wait_ge(s_pmx, 2)
            pool.wait_ge(s_csum, 1)
            pool.partition_all_reduce(rexp[:, 0, 0:3], small[:, 8:11], P, bass.bass_isa.ReduceOp.max).then_inc(s_par, 1)


            def maximum(c, i):
                pool.wait_ge(s_wsum, tval(c, i, 1))
                pool.nop(nofuse=True)
                b = c % 2
                pool.partition_all_reduce(small[:, 14 + b:15 + b], small[:, 12 + b:13 + b], P,
                                          bass.bass_isa.ReduceOp.max).then_inc(s_war, 1)

            def low(c, i):
                hi, src = w_views(c, i, HI)
                lo, _ = w_views(c, i, LO)
                pool.wait_ge(s_whi, tval(c, i, 1))
                pool.nop(nofuse=True)
                pool.tensor_tensor(lo, src, hi, ALU.subtract).then_inc(s_wfree, 1)

            def step(c, i=None):
                if c + 1 < QN:
                    maximum(c + 1, i)
                low(c, i)
                if c == QN - 3:
                    pool.wait_ge(s_wfree, QN - 2)
                    pool.memset(stage[HR:P, 0, (KH - 1) * D:KH * D], 0.0).then_inc(s_pad, 1)

            maximum(0, None)
            for c in range(0, 3):
                step(c)
            with pool.Fori(0, 4) as i:
                for c in range(3, 9):
                    step(c, i)
            for c in range(QN - 3, QN):
                step(c)

            pool.wait_ge(s_wfree, QN)
            pool.memset(ones16, 1.0).then_inc(s_z, 1)
            pool.wait_ge(s_z, 3)
            pool.affine_select(out=upper16, in_=ones16, compare_op=ALU.is_gt, fill=0.0, base=0,
                               pattern=[[1, P]], channel_multiplier=-1).then_inc(s_const, 1)
            pool.iota(pay[:, :, :, 0].bitcast(I32), [[P, T], [0, 2]], base=0, channel_multiplier=1).then_inc(s_const, 1)
            pool.memset(pay[:, :, :, 3], 0.0).then_inc(s_const, 1)
            pool.wait_ge(s_meta0, 16)
            pool.wait_ge(s_const, 10)
            pool.wait_ge(s_pay, 2)
            for t in range(T):
                for k in range(2):
                    pool.indirect_dma_start(
                        out=meta_dram, out_offset=bass.IndirectOffsetOnAxis(ap=pos[:, t, k:k + 1], axis=0),
                        in_=pay[:, t, k, :], in_offset=None).then_inc(s_scat, 16)
            pool.wait_ge(s_scat, 16 * 2 * T)
            pool.dma_start(meta[:, :, :], meta_dram[0:ET * P, :].rearrange("(j p) c -> p j c", p=P)).then_inc(s_metain, 16)
            pool.wait_ge(s_metain, 16)
            pool.wait_ge(s_hst, 16 * T)

            def gather_h(s):
                pool.wait_ge(s_fth, s.h - 1)
                col = meta[:, s.j, 0:1] if isinstance(s.j, int) else \
                    meta[:, ds(s.j, 1), 0:1].rearrange("p a c -> p (a c)")
                pool.tensor_copy(idx[:, s.hpar:s.hpar + 1], col.bitcast(I32)).then_inc(s_ix, 1)
                pool.wait_ge(s_ix, s.j + 1)
                pool.nop(nofuse=True)
                pool.indirect_dma_start(
                    out=hin[:, s.hpar, :, :].rearrange("p a d -> p (a d)"), out_offset=None, in_=h_dram,
                    in_offset=bass.IndirectOffsetOnAxis(ap=idx[:, s.hpar:s.hpar + 1], axis=0)
                ).then_inc(s_hgat[s.hpar], 16)

            gather_h(Slot(N1))
            with pool.Fori(0, (ET - 1) // 2) as i:
                for c in range(N1 + 1, N1 + 3):
                    gather_h(Slot(c, i))

            pool.wait_ge(s_yst[0], 16 * ((ET + 1) // 2))
            pool.wait_ge(s_yst[1], 16 * (ET // 2))

            def rows_of(t, gathered, cols, i, s_idx, before, landed):
                for k in range(2):
                    col_ = pos[:, t, k:k + 1] if i is None else \
                        pos[:, ds(t, 1), k:k + 1].rearrange("p a c -> p (a c)")
                    pool.tensor_copy(posb[:, cols + k:cols + k + 1], col_).then_inc(s_idx, 1)
                pool.wait_ge(s_idx, 2 + 2 * before)
                pool.nop(nofuse=True)
                for k in range(2):
                    pool.indirect_dma_start(
                        out=gathered[k], out_offset=None, in_=y_dram,
                        in_offset=bass.IndirectOffsetOnAxis(ap=posb[:, cols + k:cols + k + 1], axis=0)
                    ).then_inc(landed, 16)

            def add_rows(t, total, gathered, i, s_sum, before, stored):
                pool.tensor_tensor(total, total, gathered[0], ALU.add).then_inc(s_sum, 1)
                pool.wait_ge(s_sum, 1 + 2 * before)
                pool.tensor_tensor(total, total, gathered[1], ALU.add).then_inc(s_sum, 1)
                pool.wait_ge(s_sum, 2 + 2 * before)
                pool.nop(nofuse=True)
                dst = out_rows[t] if i is None else out_rows[ds(t, 1)].rearrange("a p d -> (a p) d")
                pool.dma_start(dst, total).then_inc(stored, 16)

            def fetch_late(k, i=None):
                b = (S1T + k) % 2
                rows_of(tval(S1T + k, i, 0, 2), [gat[:, b, 0, :], gat[:, b, 1, :]], 2 * b, i, s_ixl,
                        tval(k, i, 0, 2), s_g[b])

            def sum_late(k, i=None):
                b = (S1T + k) % 2
                pool.wait_ge(s_g[b], tval(k // 2, i, 1, 1) * 32)
                pool.wait_ge(s_acc, 2 + 2 * tval(S1T + k, i, 0, 2))
                add_rows(tval(S1T + k, i, 0, 2), acc[:, b, :], [gat[:, b, 0, :], gat[:, b, 1, :]], i, s_addl,
                         tval(k, i, 0, 2), s_out[b])

            def fetch_early(k, i=None):
                t = tval(k, i, 0, 1)
                if k:
                    pool.wait_ge(s_oute, t * 16)
                    pool.nop(nofuse=True)
                src = part_tiles[t] if i is None else part_tiles[ds(t, 1)].rearrange("a p d -> (a p) d")
                pool.dma_start(part[:, :], src).then_inc(s_pld, 16)
                rows_of(t, [yout[:, 0, :], yout[:, 1, :]], 4, i, s_ixe, t, s_ge)

            def sum_early(k, i=None):
                t = tval(k, i, 0, 1)
                pool.wait_ge(s_ge, 32 * tval(k, i, 1, 1))
                pool.wait_ge(s_pld, 16 * tval(k, i, 1, 1))
                add_rows(t, part[:, :], [yout[:, 0, :], yout[:, 1, :]], i, s_adde, t, s_oute)

            def round_(i, early):
                fetch_late(1, i)
                if early:
                    fetch_early(1, i)
                sum_late(0, i)
                fetch_late(2, i)
                if early:
                    sum_early(1, i)
                sum_late(1, i)

            rounds = (T - S1T - 1) // 2
            pool.wait_ge(s_pst[0], 16 * ((S1T + 1) // 2))
            pool.wait_ge(s_pst[1], 16 * (S1T // 2))
            fetch_early(0)
            fetch_late(0)
            sum_early(0)
            with pool.Fori(0, S1T - 1) as i:
                round_(i, True)
            if rounds > S1T - 1:
                with pool.Fori(S1T - 1, rounds) as i:
                    round_(i, False)
            sum_late(T - S1T - 1)
            pool.wait_ge(s_out[0], 16 * (T // 2 - (S1T + 1) // 2))
            pool.wait_ge(s_out[1], 16 * (T // 2 - S1T // 2))
            pool.wait_ge(s_oute, 16 * S1T)

        @block.scalar
        def _(a):
            def sum_w(c, i):
                signal, count = landed(c, i)
                a.wait_ge(signal, count)
                if c % 3 == DOWN:
                    a.wait_ge(s_pad, 2 if c == QN - 1 else 1)
                if c == QN - 1:
                    a.wait_ge(s_wfree, QN - 3)
                a.nop(nofuse=True)
                dst, src = w_views(c, i, HI)
                nc.scalar.activation(dst, src, ACT.Abs,
                                     accum_out=small[:, 12 + c % 2:13 + c % 2]).then_inc(s_wsum, 1)

            def split_w(c, i):
                a.wait_ge(s_wss, tval(c, i, 1))
                a.nop(nofuse=True)
                dst, src = w_views(c, i, HI)
                nc.scalar.activation(dst, src, ACT.Copy).then_inc(s_whi, 1)

            def step(c, i=None):
                t = tval(c, i)
                if 0 <= c + 1 < T:
                    a.wait_ge(s_tx, tval(c, i, 2))
                    nc.scalar.activation(xt[:, (c + 1) % 2, :, :, :], p_tx, ACT.Copy).then_inc(s_xt, 1)
                if 0 <= c + 2 < T:
                    a.wait_ge(s_xsc, tval(c, i, 3))
                    if c == -2:
                        a.wait_ge(s_meta0, 16)
                    nc.scalar.activation(x16[:, HI, :], xrow[:, c % 2, :], ACT.Copy,
                                         scale=small[:, 2 + c % 2:3 + c % 2]).then_inc(s_xhi, 1)
                if 0 <= c < QN:
                    sum_w(c, i)
                if 0 <= c - 1 < T:
                    a.wait_ge(s_th, tval(c, i))
                    nc.scalar.activation(xt[:, c % 2, :, :, :], p_th, ACT.Copy).then_inc(s_ht, 1)
                if 0 <= c - 1 < QN:
                    split_w(c - 1, i)
                if 0 <= c < T:
                    a.wait_ge(s_hsc, tval(c, i, 1))
                    if c >= 1:
                        a.wait_ge(s_hst, tval(c, i) * 16)
                    nc.scalar.activation(h16[:, HI, :], p_h[c % 2], ACT.Copy, scale=small[:, 7:8]).then_inc(s_hhi, 1)

            a.wait_ge(s_cw, 16)
            w_src = stage[:, :, :].rearrange("p b n -> p (b n)")
            nc.scalar.activation(cw[:, :, HI, :], w_src[:, 0:KD * D].rearrange("p (k d) -> p k d", k=KD), ACT.Abs,
                                 accum_out=small[:, 8:9]).then_inc(s_csum, 1)
            step(-2)
            a.wait_ge(s_pc, 2)
            for k in range(KD + 1):
                a.wait_ge(s_pt, k + 1)
                dst = cw[:, k, HI, :] if k < KD else lat[:, :, HI, :]
                src = ps[:, 1 + k, :] if k < KD else ps[:, 1 + k, :].rearrange("p (k n) -> p k n", k=KD)
                part = 0 if k < KD else 1
                nc.scalar.activation(dst, src, ACT.Copy, scale=rexp[:, 2, part:part + 1]).then_inc(s_phi, 1)
            a.wait_ge(s_pt, KD + 2)
            nc.scalar.activation(lbt[:, :], ps[:, KD + 2, :], ACT.Copy).then_inc(s_phi, 1)
            nc.scalar.activation(wr[:, :, HI, :], wr32, ACT.Copy, scale=rexp[:, 2, 2:3]).then_inc(s_phi, 1)

            for c in range(-1, 4):
                step(c)
            with a.Fori(0, 4) as i:
                for c in range(4, 10):
                    step(c, i)
            for c in range(28, T + 1):
                step(c)

            a.wait_ge(s_rd, 1)
            nc.scalar.activation(r_s, r_s, ACT.Exp).then_inc(s_re, 1)

            def slot(s, prev):
                if s and s.last and s.c < NS - 1:
                    a.wait_ge(s_fth, s.h + 2)
                    nc.scalar.activation(ht[:, 1 - s.hpar, :, :, :], p_fth, ACT.Copy).then_inc(s_fht, 1)
                if prev:
                    a.wait_ge(s_ta, prev.n + 1)
                    nc.scalar.activation(at[:, prev.par, :, :, :], p_at, ACT.Copy).then_inc(s_at, 1)
                if s:
                    a.wait_ge(s_gu, s.n + 1)
                    if s.c == 0:
                        a.wait_ge(s_coef, 12)
                    if s.c == N1:
                        a.wait_ge(s_coef, 15)
                    nc.scalar.activation(act[:, :], p_g[s.par], ACT.Silu, scale=col(cg, s.n)).then_inc(s_silu, 1)
                    a.wait_ge(s_asc, s.n + 1)
                    nc.scalar.activation(a16[:, HI, :], act[:, :], ACT.Copy, scale=fsm[:, 2:3]).then_inc(s_ahi, 1)
                if prev and not prev.shared:
                    a.wait_ge(s_dn, prev.n + 1)
                    a.wait_ge(s_cy, prev.n + 1)
                    if prev.c >= N1 + 2:
                        a.wait_ge(s_yst[prev.par], yst_before(prev))
                    nc.scalar.activation(yout[:, prev.par, :], p_y[prev.par], ACT.Copy,
                                         scale=col(cy, prev.n)).then_inc(s_y, 1)

            a.wait_ge(s_fth, 1)
            nc.scalar.activation(ht[:, 0, :, :, :], p_fth, ACT.Copy).then_inc(s_fht, 1)
            run_slots(a, slot)
            tail(slot)

        @block.vector
        def _(v):
            V = nc.vector

            def row_max(o, src, axis=AX):
                return V.tensor_reduce(o, src, axis, ALU.max, apply_absolute_value=True)

            def exponent(o, amax):
                return V.tensor_scalar(o.bitcast(I32), amax.bitcast(I32), EXP_MASK, None, ALU.bitwise_and)

            def inverse(o, ex):
                return V.tensor_scalar(o.bitcast(I32), ex.bitcast(I32), float(MIN_EXP * ONE_EXP),
                                       float(-TOP * ONE_EXP), ALU.max, ALU.add)

            def scale_of(o, inv):
                return V.tensor_scalar(o.bitcast(I32), inv.bitcast(I32), -1.0, float(254 * ONE_EXP),
                                       ALU.mult, ALU.add)

            def scale_from(o, ex):
                return V.scalar_tensor_tensor(out=o.bitcast(I32), in0=scale_c[:, 0:1], scalar=ex.bitcast(I32),
                                              in1=scale_c[:, 1:2], op0=ALU.subtract, op1=ALU.min)

            def max_x(c, i):
                v.wait_ge(s_xld[(c + 1) % 2], tval((c + 3) // 2, i, 1, 3) * 16)
                row_max(small[:, 0:1], xrow[:, (c + 1) % 2, :]).then_inc(s_xmx, 1)

            def step(c, i=None):
                def tab(table, k):
                    n = tval(c, i, k)
                    return col(table, n)
                x_, w_ = 0 <= c + 2 < T, 0 <= c - 1 < QN
                if x_:
                    nx = tval(c, i, 3)
                    v.wait_ge(s_xmx, nx)
                    exponent(small[:, 1:2], small[:, 0:1]).then_inc(s_xex, 1)
                if w_:
                    kind, e = chunk(c - 1, i)
                    nw = tval(c, i)
                    v.wait_ge(s_war, nw)
                    exponent(small[:, 8:9], small[:, 15 - c % 2:16 - c % 2]).then_inc(s_wex, 1)
                if x_:
                    v.wait_ge(s_xex, nx)
                    scale_from(small[:, 2 + c % 2:3 + c % 2], small[:, 1:2]).then_inc(s_xsc, 1)
                    inverse(tab(xinv, 2), small[:, 1:2]).then_inc(s_xiv, 1)
                if w_:
                    v.wait_ge(s_wex, nw)
                    scale_from(small[:, 9:10], small[:, 8:9]).then_inc(s_wsc, 1)
                    inv = winv[:, kind, e:e + 1] if isinstance(e, int) else winv[:, kind, ds(e, 1)]
                    inverse(inv, small[:, 8:9]).then_inc(s_wiv, 1)
                    v.wait_ge(s_wsc, nw)
                    _, src = w_views(c - 1, i, HI)
                    V.tensor_scalar(src, src, small[:, 9:10], None, ALU.mult).then_inc(s_wss, 1)
                if 0 <= c < T:
                    v.wait_ge(s_xa, tval(c, i, 1))
                    V.tensor_scalar(xam[:, :], p_xa, col(lmask, tval(c // 2, i, 0, 3)), None,
                                    ALU.mult).then_inc(s_xam, 1)
                if x_:
                    v.wait_ge(s_xhi, nx)
                    V.scalar_tensor_tensor(out=x16[:, LO, :], in0=xrow[:, c % 2, :],
                                           scalar=small[:, 2 + c % 2:3 + c % 2], in1=x16[:, HI, :],
                                           op0=ALU.mult, op1=ALU.subtract).then_inc(s_xlo, 1)
                if 0 <= c < T:
                    n = tval(c, i, 1)
                    v.wait_ge(s_h, n)
                    row_max(small[:, 4:5], p_h[c % 2]).then_inc(s_hmx, 1)
                if 0 <= c - 1 < T:
                    v.wait_ge(s_rt, tval(c, i))
                    V.tensor_scalar(rlog[:, :, :].rearrange("p a e -> p (a e)"), p_rt, tab(ch, -1), rexp[:, 1, 2:3],
                                    ALU.mult, ALU.mult).then_inc(s_rlog, 1)
                if 0 <= c < T:
                    v.wait_ge(s_hmx, n)
                    exponent(small[:, 5:6], small[:, 4:5]).then_inc(s_hex, 1)
                    v.wait_ge(s_hex, n)
                    scale_from(small[:, 7:8], small[:, 5:6]).then_inc(s_hsc, 1)
                    inverse(small[:, 6:7], small[:, 5:6]).then_inc(s_hiv, 1)
                if 0 <= c - 1 < T:
                    v.wait_ge(s_rlog, tval(c, i))
                    t1 = tval(c, i, -1)
                    dst = logits[:, t1, :] if i is None else logits[:, ds(t1, 1), :].rearrange("p a e -> p (a e)")
                    V.tensor_tensor(dst, rlog[:, 0, :], rlog[:, 1, :], ALU.add).then_inc(s_log, 1)
                if 0 <= c + 3 < T:
                    max_x(c, i)
                if 0 <= c < T:
                    v.wait_ge(s_hiv, n)
                    v.wait_ge(s_xiv, n)
                    V.tensor_scalar(tab(ch, 0), small[:, 6:7], tab(xinv, 0), rexp[:, 1, 0:1],
                                    ALU.mult, ALU.mult).then_inc(s_ch, 1)
                    v.wait_ge(s_hhi, n)
                    V.scalar_tensor_tensor(out=h16[:, LO, :], in0=p_h[c % 2], scalar=small[:, 7:8],
                                           in1=h16[:, HI, :], op0=ALU.mult, op1=ALU.subtract).then_inc(s_hlo, 1)
                    v.wait_ge(s_ch, n)

            w_src = stage[:, :, :].rearrange("p b n -> p (b n)")
            v.wait_ge(s_la, 16 * 2)
            row_max(small[:, 9:10], w_src[:, KD * D:KD * D + D]).then_inc(s_pmx, 1)
            row_max(small[:, 10:11], early[:, P:P + KD * E]).then_inc(s_pmx, 1)
            max_x(-3, None)
            v.wait_ge(s_const, 7)
            step(-2)
            v.wait_ge(s_par, 1)
            exponent(rexp[:, 1, 0:3], rexp[:, 0, 0:3]).then_inc(s_plo, 1)
            v.wait_ge(s_plo, 1)
            inverse(rexp[:, 1, 0:3], rexp[:, 1, 0:3]).then_inc(s_pc, 1)
            v.wait_ge(s_pc, 1)
            scale_of(rexp[:, 2, 0:3], rexp[:, 1, 0:3]).then_inc(s_pc, 1)
            v.wait_ge(s_pin, 16 * (2 + KD))
            V.tensor_scalar(pcol[:, 1:2].bitcast(I32), pcol[:, 1:2].bitcast(I32), RANK.bit_length() - 1, None,
                            ALU.arith_shift_right).then_inc(s_pc, 1)
            V.tensor_copy(lmask[:, :], lmask[:, :].bitcast(I32)).then_inc(s_pc, 1)
            v.wait_ge(s_pc, 4)
            V.tensor_copy(pcol[:, 2:3], pcol[:, 1:2].bitcast(I32)).then_inc(s_pc, 1)
            V.tensor_scalar(pcol[:, 3:4], pcol[:, 0:1], rexp[:, 2, 0:1], rexp[:, 1, 1:2],
                            ALU.mult, ALU.mult).then_inc(s_pc, 1)
            v.wait_ge(s_pc, 6)
            V.tensor_scalar(lmask[:, :], lmask[:, :], pcol[:, 2:3], pcol[:, 3:4],
                            ALU.is_equal, ALU.mult).then_inc(s_pc, 1)
            for k in range(KD + 1):
                v.wait_ge(s_phi, k + 1)
                hi, lo = (cw[:, k, HI, :], cw[:, k, LO, :]) if k < KD else (lat[:, :, HI, :], lat[:, :, LO, :])
                src = ps[:, 1 + k, :] if k < KD else ps[:, 1 + k, :].rearrange("p (k n) -> p k n", k=KD)
                c_ = 0 if k < KD else 1
                V.scalar_tensor_tensor(out=lo, in0=src, scalar=rexp[:, 2, c_:c_ + 1], in1=hi,
                                       op0=ALU.mult, op1=ALU.subtract).then_inc(s_plo, 1)
            v.wait_ge(s_phi, KD + 3)
            V.scalar_tensor_tensor(out=wr[:, :, LO, :], in0=wr32, scalar=rexp[:, 2, 2:3],
                                   in1=wr[:, :, HI, :], op0=ALU.mult, op1=ALU.subtract).then_inc(s_plo, 1)

            for c in range(-1, 4):
                step(c)
            with v.Fori(0, 4) as i:
                for c in range(4, 10):
                    step(c, i)
            for c in range(28, T + 1):
                step(c)

            chain = [0]

            def link(ins):
                chain[0] += 1
                ins.then_inc(s_r, 1)
                v.wait_ge(s_r, chain[0])

            def by_t(a_):
                return a_.unsqueeze(2).broadcast_to([P, T, E])

            def by_e(a_, n=T):
                return a_.unsqueeze(1).broadcast_to([P, n, E])

            v.wait_ge(s_log, T)
            v.wait_ge(s_wfree, QN)
            link(V.tensor_reduce(r_max, logits[:, :, :], AX, ALU.max))
            V.tensor_tensor(te(r_s), logits[:, :, :], by_t(r_max), ALU.subtract).then_inc(s_rd, 1)
            for half in range(2):
                for base, t0, t1 in ((0, 0, S1T), (ET, S1T, T)):
                    for table, kind in ((cg, GATE), (cu, UP), (cd, DOWN)):
                        sel = table[:, base + 2 * t0:base + 2 * t1].rearrange("p (t s) -> p t s", s=2)[:, :, half]
                        w_ = winv[:, kind, E + half:E + half + 1]
                        if kind == DOWN:
                            V.tensor_copy(sel, w_.broadcast_to([P, t1 - t0])).then_inc(s_coef, 1)
                        else:
                            V.tensor_scalar(sel, ch[:, t0:t1], w_, None, ALU.mult).then_inc(s_coef, 1)
            v.wait_ge(s_coef, 12)

            def pick(scores, value, lowest, onehot):
                link(V.tensor_reduce(value, te(scores), AX, ALU.max))
                link(V.tensor_tensor(te(r_eq), te(scores), by_t(value), ALU.is_equal))
                link(V.scalar_tensor_tensor(out=te(r_cand), in0=te(r_eq), scalar=float(-E), in1=by_e(iota_e[:, :]),
                                            op0=ALU.mult, op1=ALU.add))
                link(V.tensor_reduce(lowest, te(r_cand), AX, ALU.min))
                link(V.tensor_tensor(te(onehot), te(r_cand), by_t(lowest), ALU.is_equal))


            totals = []

            def route_first():
                v.wait_ge(s_re, 1)
                link(V.tensor_reduce(r_sum, te(r_s), AX, ALU.add))
                link(V.reciprocal(r_sum, r_sum))
                link(V.tensor_tensor(te(r_s), te(r_s), by_t(r_sum), ALU.mult))

                pick(r_s, r_v1, r_e1, r_oh1)

            def route_second():
                link(V.scalar_tensor_tensor(out=r_s2, in0=r_oh1, scalar=-2.0, in1=r_s, op0=ALU.mult, op1=ALU.add))
                pick(r_s2, r_v2, r_e2, r_oh2)
                V.tensor_tensor(m16, r_oh1, r_oh2, ALU.add).then_inc(s_m16, 1)
                v.wait_ge(s_const, 10)
                for k, val in ((0, r_v1), (1, r_v2)):
                    link(V.tensor_copy(pay[:, :, k, 1], ch[:, :]))
                    link(V.tensor_copy(pay[:, :, k, 2], val))

            def route_counts():
                v.wait_ge(s_rmm, 1)
                V.tensor_copy(r_cs, p_count).then_inc(s_rcp, 1)
                V.tensor_copy(r_cand, p_rank).then_inc(s_rcp, 1)
                v.wait_ge(s_rcp, 2)
                src, dst = r_cs, r_in0
                d_ = 1
                while d_ < T:
                    link(V.tensor_tensor(dst[:, d_ * E:TE], src[:, d_ * E:TE], src[:, 0:TE - d_ * E], ALU.add))
                    link(V.tensor_copy(dst[:, 0:d_ * E], src[:, 0:d_ * E]))
                    src, dst = dst, (r_in1 if dst is r_in0 else r_in0)
                    d_ *= 2
                totals.append((src, dst))

            def route_places():
                src, dst = totals[0]
                link(V.tensor_scalar(r_n, src[:, TE - E:TE], float(P - 1), None, ALU.add))
                link(V.tensor_copy(r_tmp.bitcast(I32), r_n))
                link(V.tensor_scalar(r_tmp.bitcast(I32), r_tmp.bitcast(I32), P.bit_length() - 1, None,
                                     ALU.arith_shift_right))
                link(V.tensor_copy(r_tiles, r_tmp.bitcast(I32)))
                link(V.tensor_copy(r_end, r_tiles))
                for e in range(1, E):
                    link(V.tensor_tensor(r_end[:, e:e + 1], r_end[:, e:e + 1], r_end[:, e - 1:e], ALU.add))
                link(V.tensor_tensor(r_base, r_end, r_tiles, ALU.subtract))
                link(V.tensor_scalar(r_base, r_base, float(P), None, ALU.mult))
                link(V.tensor_tensor(dst, src, r_cs, ALU.subtract))
                link(V.tensor_tensor(dst, dst, r_cand, ALU.add))
                link(V.tensor_tensor(te(dst), te(dst), by_e(r_base), ALU.add))
                for k, onehot in ((0, r_oh1), (1, r_oh2)):
                    link(V.tensor_tensor(r_eq, onehot, dst, ALU.mult))
                    link(V.tensor_reduce(r_e1, te(r_eq), AX, ALU.add))
                    V.tensor_copy(pos[:, :, k], r_e1).then_inc(s_pay, 1)
                    v.wait_ge(s_pay, k + 1)

            def route_tiles():
                ej = [P, ET, E]
                link(V.tensor_tensor(j_a, iota_j[:, :].unsqueeze(2).broadcast_to(ej), r_end.unsqueeze(1).broadcast_to(ej),
                                     ALU.is_ge))
                link(V.tensor_reduce(r_in1[:, 0:ET], j_a, AX, ALU.add))
                link(V.tensor_scalar(r_in1[:, 0:ET], r_in1[:, 0:ET], float(E - 1), None, ALU.min))
                V.tensor_copy(etile[:, :], r_in1[:, 0:ET]).then_inc(s_et, 1)
                link(V.tensor_tensor(j_a, iota_e[:, :].unsqueeze(1).broadcast_to(ej), r_in1[:, 0:ET].unsqueeze(2).broadcast_to(ej),
                                     ALU.is_equal))
                for table, kind in ((cg, GATE), (cu, UP), (cd, DOWN)):
                    link(V.tensor_tensor(j_b, j_a, winv[:, kind, 0:E].unsqueeze(1).broadcast_to(ej), ALU.mult))
                    link(V.tensor_reduce(table[:, N1:N2], j_b, AX, ALU.add))


            def beside(c):
                if c == 0:
                    route_first()
                if c == 1:
                    route_second()
                if c == 3:
                    route_counts()
                if c == 4:
                    route_places()
                if c == 5:
                    route_tiles()

            def slot(s, prev):
                if s and s.c == N1:
                    v.wait_ge(s_metain, 16)
                    for table, k in ((cg, 1), (cu, 1), (cd, 2)):
                        V.tensor_tensor(table[:, N1:N2], table[:, N1:N2], meta[:, :, k], ALU.mult).then_inc(s_coef, 1)
                    v.wait_ge(s_coef, 15)
                if s:
                    n = s.n + 1
                    v.wait_ge(s_silu, n)
                    V.scalar_tensor_tensor(out=act[:, :], in0=p_u[s.par], scalar=col(cu, s.n), in1=act[:, :],
                                           op0=ALU.mult, op1=ALU.mult).then_inc(s_a, 1)
                    v.wait_ge(s_a, n)
                    row_max(fsm[:, 0:1], act[:, :]).then_inc(s_amx, 1)
                    v.wait_ge(s_amx, n)
                    exponent(fsm[:, 0:1], fsm[:, 0:1]).then_inc(s_aex, 1)
                    v.wait_ge(s_aex, n)
                    scale_from(fsm[:, 2:3], fsm[:, 0:1]).then_inc(s_asc, 1)
                    inverse(fsm[:, 1:2], fsm[:, 0:1]).then_inc(s_aiv, 1)
                    v.wait_ge(s_aiv, n)
                    V.tensor_tensor(col(cy, s.n), fsm[:, 1:2], col(cd, s.n), ALU.mult).then_inc(s_cy, 1)
                    v.wait_ge(s_ahi, n)
                    V.scalar_tensor_tensor(out=a16[:, LO, :], in0=act[:, :], scalar=fsm[:, 2:3], in1=a16[:, HI, :],
                                           op0=ALU.mult, op1=ALU.subtract).then_inc(s_alo, 1)
                if prev and prev.shared:
                    v.wait_ge(s_dn, prev.n + 1)
                    v.wait_ge(s_cy, prev.n + 1)
                    if prev.half == 0:
                        v.wait_ge(s_xin[prev.tpar], 16 * (prev.tq + 1))
                    else:
                        v.wait_ge(s_acc, prev.k)
                    V.scalar_tensor_tensor(out=acc[:, prev.tpar, :], in0=p_y[prev.par], scalar=col(cy, prev.n),
                                           in1=acc[:, prev.tpar, :], op0=ALU.mult, op1=ALU.add).then_inc(s_acc, 1)

            run_slots(v, slot, beside)
            tail(slot)

        @block.tensor
        def _(pe):
            w_src = stage[:, :, :].rearrange("p b n -> p (b n)")
            pe.wait_ge(s_cw, 16)
            pe.wait_ge(s_const, 1)
            for k in range(KD):
                for c in range(KD):
                    mm = pe.transpose(ps[:, 1 + k, c * P:(c + 1) * P], w_src[:, c * D + k * P:c * D + (k + 1) * P],
                                      ident)
                mm.then_inc(s_pt, 1)
            pe.wait_ge(s_la, 16 * 2)
            pe.wait_ge(s_pin, 16 * (2 + KD))
            for j in range(2):
                for c in range(KD):
                    o = KD * D + j * D + c * P
                    mm = pe.transpose(ps[:, 1 + KD + j, c * P:(c + 1) * P], w_src[:, o:o + P], ident)
                mm.then_inc(s_pt, 1)

            def split_matmul(dst, lhs, rhs, n, stop):
                parts = [(k, a_, b_) for k in range(n) for a_, b_ in ((HI, HI), (HI, LO), (LO, HI))]
                for m, (k, a_, b_) in enumerate(parts):
                    mm = pe.matmul(dst, lhs(k, a_), rhs(k, b_), start=(m == 0), stop=(stop and m == len(parts) - 1))
                return mm

            def transpose_halves(dst, rows):
                for a_ in (HI, LO):
                    for k in range(KD):
                        mm = pe.transpose(dst[:, a_, k, :], rows[:, a_, k * P:(k + 1) * P], ident16[:, :])
                return mm

            def step(c, i=None):
                b = c % 2
                if 0 <= c + 1 < T:
                    pe.wait_ge(s_xlo, tval(c, i, 2))
                    if c >= 0:
                        pe.wait_ge(s_xt, tval(c, i, 1))
                    transpose_halves(p_tx, x16).then_inc(s_tx, 1)
                if c == 0:
                    pe.wait_ge(s_phi, KD + 3)
                    pe.wait_ge(s_plo, KD + 3)
                if 0 <= c < T:
                    pe.wait_ge(s_xt, tval(c, i, 1))
                    if c >= 1:
                        pe.wait_ge(s_xam, tval(c, i))
                    split_matmul(p_xa, lambda k, a_: lat[:, k, a_, :], lambda k, b_: xt[:, b, b_, k, :],
                                 KD, True).then_inc(s_xa, 1)
                    if c >= 2:
                        pe.wait_ge(s_hlo, tval(c, i, -1))
                    split_matmul(p_h[b], lambda k, a_: xt[:, b, a_, k, :], lambda k, b_: cw[:, k, b_, :], KD, False)
                if 0 <= c - 1 < T:
                    pe.wait_ge(s_hlo, tval(c, i))
                    if c >= 2:
                        pe.wait_ge(s_ht, tval(c, i, -1))
                    transpose_halves(p_th, h16).then_inc(s_th, 1)
                if 0 <= c < T:
                    pe.wait_ge(s_xam, tval(c, i, 1))
                    pe.matmul(p_h[b], xam[:, :], lbt[:, :], start=False, stop=True).then_inc(s_h, 1)
                if 0 <= c - 1 < T:
                    pe.wait_ge(s_ht, tval(c, i))
                    if c >= 2:
                        pe.wait_ge(s_log, tval(c, i, -1))
                    for k in range(KD):
                        for a_ in (HI, LO):
                            mm = pe.matmul(p_rt, xt[:, b, a_, k, :], wr[:, k, :, :].rearrange("p a e -> p (a e)"),
                                           start=(k == 0 and a_ == HI), stop=(k == KD - 1 and a_ == LO))
                    mm.then_inc(s_rt, 1)

            for c in range(-1, 4):
                step(c)
            with pe.Fori(0, 4) as i:
                for c in range(4, 10):
                    step(c, i)
            for c in range(28, T + 1):
                step(c)

            def beside(c):
                if c == 3:
                    pe.wait_ge(s_m16, 1)
                    pe.wait_ge(s_const, 10)
                    pe.wait_ge(s_fht, 3)
                    pe.matmul(p_rank, upper16, m16, start=True, stop=True)
                    pe.matmul(p_count, ones16, m16, start=True, stop=True).then_inc(s_rmm, 1)
                if c == 4:
                    pe.wait_ge(s_rcp, 2)

            def transpose_rows(hc, i):
                hpar = hc % 2
                if hc < H1:
                    landed, count = s_hin, hc // 2 + 1
                elif hc < H2:
                    landed, count = s_hgat, (hc - H1) // 2 + 1
                else:
                    landed, count = s_hin, (H1 + 1 - hpar) // 2 + (hc - H2) // 2 + 1
                pe.wait_ge(landed[hpar], tval(count, i, 0, 1) * 16)
                transpose_halves(p_fth, hin[:, hpar, :, :]).then_inc(s_fth, 1)

            def weights(w, s, e, k, half):
                if s.shared:
                    return w[:, s.expert, k, half, :]
                return w[:, ds(e, 1), k, half, :].rearrange("p a n -> p (a n)")

            def expert_of(s):
                if s.shared:
                    return None
                o = etile[0:1, s.j:s.j + 1] if isinstance(s.j, int) else etile[0:1, ds(s.j, 1)]
                return pe.value_load(o, min_val=0, max_val=E - 1)

            def slot(s, prev):
                if s:
                    if s.c == N1:
                        pe.wait_ge(s_et, 1)
                    e = expert_of(s)
                    if s.last and s.c < NS - 1:
                        pe.wait_ge(s_fht, s.h + 1)
                        transpose_rows(s.hc + 1, s.i)
                    pe.wait_ge(s_fht, s.h + 1)
                    if s.c >= 2:
                        pe.wait_ge(s_silu, s.n - 1)
                        pe.wait_ge(s_a, s.n - 1)
                    for k in range(KD):
                        for wh in (HI, LO):
                            for w, dst in ((wg, p_g), (wu, p_u)):
                                pe.matmul(dst[s.par], ht[:, s.hpar, HI, k, :], weights(w, s, e, k, wh),
                                          start=(k == 0 and wh == HI), stop=False)
                if prev:
                    pe.wait_ge(s_alo, prev.n + 1)
                    if prev.c >= 1:
                        pe.wait_ge(s_at, prev.n)
                    for a_ in (HI, LO):
                        for k in range(KH):
                            m = P if k < KH - 1 else HR
                            mm = pe.transpose(p_at[0:m, a_, k, :], a16[:, a_, k * P:k * P + m], ident16[:, :])
                    mm.then_inc(s_ta, 1)
                if s:
                    for k in range(KD):
                        for w, dst in ((wg, p_g), (wu, p_u)):
                            mm = pe.matmul(dst[s.par], ht[:, s.hpar, LO, k, :], weights(w, s, e, k, HI),
                                           start=False, stop=(k == KD - 1))
                    mm.then_inc(s_gu, 1)
                if prev:
                    e = expert_of(prev)
                    pe.wait_ge(s_at, prev.n + 1)
                    if 2 <= prev.c < N1 + 2:
                        pe.wait_ge(s_acc, prev.n - 1)
                    elif N1 + 2 <= prev.c < N2 + 2:
                        pe.wait_ge(s_y, prev.n - 1 - N1)
                    elif prev.c >= N2 + 2:
                        pe.wait_ge(s_acc, prev.n - 1 - ET)
                    parts = [(k, a_, b_) for k in range(KH) for a_, b_ in ((HI, HI), (HI, LO), (LO, HI))]
                    for m, (k, a_, b_) in enumerate(parts):
                        rows = P if k < KH - 1 else HR
                        mm = pe.matmul(p_y[prev.par], at[0:rows, prev.par, a_, k, :], weights(wd, prev, e, k, b_)[0:rows],
                                       start=(m == 0), stop=(m == len(parts) - 1))
                    mm.then_inc(s_dn, 1)

            pe.wait_ge(s_log, T)
            pe.wait_ge(s_hlo, T)
            transpose_rows(0, None)
            run_slots(pe, slot, beside)
            tail(slot)


_INS = ['x', 'itok_B_0_6', 'L0_cond_W', 'L0_cond_A', 'L0_cond_Bm', 'L0_cond_scalings', 'L0_ffn_W_router',
        'L0_ffn_We_gate', 'L0_ffn_We_up', 'L0_ffn_We_down', 'L0_ffn_Ws_gate', 'L0_ffn_Ws_up', 'L0_ffn_Ws_down']
_OUTS = [((16, 256, 512), 'float32')]


def kernel(**inputs):
    import numpy as _np
    import concourse.bacc as _bacc
    from concourse import mybir as _mybir
    from concourse.bass_utils import run_bass_kernel_spmd as _run

    nc = _bacc.Bacc("TRN2", target_bir_lowering=False, num_devices=1)
    arrays, args = {}, []
    for name in _INS:
        a = _np.ascontiguousarray(inputs[name])
        arrays[f"in_{name}_dram"] = a
        args.append(nc.dram_tensor(f"in_{name}_dram", a.shape, _mybir.dt.from_np(a.dtype), kind="ExternalInput").ap())
    for i, (shape, dtype) in enumerate(_OUTS):
        dt = _mybir.dt.from_np(_np.dtype(dtype))
        args.append(nc.dram_tensor(f"out_{i}_dram", shape, dt, kind="ExternalOutput").ap())
    adaln_moe_kernel(nc, *args)
    r = _run(nc, [arrays], core_ids=[0])
    got = tuple(r.results[0][f"out_{i}_dram"] for i in range(len(_OUTS)))
    return got[0]
```

```python
from contextlib import ExitStack

import concourse.bass as bass
from concourse import mybir

F32, F16, I32 = mybir.dt.float32, mybir.dt.float16, mybir.dt.int32
ALU = mybir.AluOpType
ACT = mybir.ActivationFunctionType
AX = mybir.AxisListType.X

P = 128
HI, LO = 0, 1
GATE, UP, DOWN = 0, 1, 2

EXP_MASK = 0x7F800000
ONE_EXP = 1 << 23
TOP = 14
MIN_EXP = 27


def adaln_moe_kernel(nc, x, adapter_idx, cond_w, lora_a, lora_b, scalings, w_router,
                     we_gate, we_up, we_down, ws_gate, ws_up, ws_down, out):
    B, S, D = x.shape
    NA, RANK, _ = lora_a.shape
    E, _, H = we_gate.shape
    assert NA * RANK == P and ws_gate.shape[1] == 2 * H and D == 4 * P
    TOKENS = B * S
    T = TOKENS // P
    TPB = S // P
    KD = D // P
    KH = -(-H // P)
    HR = H - (KH - 1) * P
    EX = E + 2
    ET = 2 * TOKENS // P + E - 1
    S1T = 11
    LEAD = 8
    N1 = 2 * S1T
    N2 = N1 + ET
    NS = N2 + 2 * (T - S1T)
    H1 = S1T
    H2 = H1 + ET
    SLOTS = (ET + 1) * P
    assert TPB == 2 and ET % 2 == 1 and S1T % 2 == 1 and (T - S1T) % 2 == 1 and N1 % 2 == 0

    x_rows = x.rearrange("b (t p) d -> (b t) p d", p=P)
    out_rows = out.rearrange("b (t p) d -> (b t) p d", p=P)
    h_dram = nc.dram_tensor("h_dram", [TOKENS, 2 * D], F16).ap()
    y_dram = nc.dram_tensor("y_dram", [ET * P, D], F32).ap()
    part_dram = nc.dram_tensor("part_dram", [S1T * P, D], F32).ap()
    meta_dram = nc.dram_tensor("meta_dram", [SLOTS, 4], F32).ap()
    h_tiles = h_dram.rearrange("(t p) d -> t p d", p=P)
    y_tiles = y_dram.rearrange("(t p) d -> t p d", p=P)
    part_tiles = part_dram.rearrange("(t p) d -> t p d", p=P)
    ds = bass.ds

    with ExitStack() as ctx:
        def sb(name, shape, dt, c=ctx):
            return c.enter_context(nc.sbuf_tensor(name, shape, dt))

        def sem(name):
            return ctx.enter_context(nc.semaphore(name))

        wg = sb("wg", [P, EX, KD, 2, H], F16)
        wu = sb("wu", [P, EX, KD, 2, H], F16)
        wd = sb("wd", [P, EX, KH, 2, D], F16)
        ident16 = sb("ident16", [P, P], F16)
        ch = sb("ch", [P, T], F32)
        winv = sb("winv", [P, 3, EX], F32)
        iota_e = sb("iota_e", [P, E], F32)
        scale_c = sb("scale_c", [P, 2], F32)
        iota_j = sb("iota_j", [P, ET], F32)

        actx = ExitStack()
        stage = sb("stage", [P, 2, KH * D], F32, actx)
        cw = sb("cw", [P, KD, 2, D], F16, actx)
        lat = sb("lat", [P, KD, 2, P], F16, actx)
        lbt = sb("lbt", [P, D], F32, actx)
        xrow = sb("xrow", [P, 2, D], F32, actx)
        wr = sb("wr", [P, KD, 2, E], F16, actx)
        lmask = sb("lmask", [P, B], F32, actx)
        x16 = sb("x16", [P, 2, D], F16, actx)
        xt = sb("xt", [P, 2, 2, KD, P], F16, actx)
        xam = sb("xam", [P, P], F32, actx)
        xinv = sb("xinv", [P, T], F32, actx)
        small = sb("small", [P, 16], F32, actx)
        rlog = sb("rlog", [P, 2, E], F32, actx)
        rexp = sb("rexp", [P, 3, 4], F32, actx)
        h16 = sb("h16", [P, 2, D], F16, actx)
        early = h16[:, :, :].rearrange("p a d -> p (a d)").bitcast(F32)
        ident = early[:, 0:P]
        wr32 = early[:, P:P + KD * E].rearrange("p (k e) -> p k e", k=KD)
        pcol = early[:, P + KD * E:P + KD * E + 4]
        actx.close()
        stage_down = wd[:, E, :, :, :].rearrange("p k a d -> p (k a d)").bitcast(F32)

        low = sb("low", [P, 2, KH * D], F32)
        ht = [low[:, b, o:o + D].bitcast(F16).rearrange("p (a k n) -> p a k n", a=2, k=KD)
              for b, o in ((1, 0), (0, 0))]
        hin = low[:, 1, D:3 * D].bitcast(F16).rearrange("p (b a d) -> p b a d", b=2, a=2)
        act = low[:, 0, D:D + H]
        a16 = low[:, 0, D + H:D + 2 * H].bitcast(F16).rearrange("p (a h) -> p a h", a=2)
        route = sb("route", [P, 3072], F32)
        cg = sb("cg", [P, NS], F32)
        cu = sb("cu", [P, NS], F32)
        cd = sb("cd", [P, NS], F32)
        cy = sb("cy", [P, NS], F32)
        fsm = sb("fsm", [P, 4], F32)
        idx = sb("idx", [P, 2], I32)
        posb = sb("posb", [P, 6], I32)
        at = sb("at", [P, 2, 2, KH, P], F16)
        acc = sb("acc", [P, 2, D], F32)
        meta = sb("meta", [P, ET, 4], F32)
        pos = sb("pos", [P, T, 2], I32)
        etile = sb("etile", [P, ET], I32)
        part = sb("part", [P, D], F32)
        yout = route[:, 0:2 * D].rearrange("p (b d) -> p b d", b=2)
        gat = route[:, 2 * D:6 * D].rearrange("p (b s d) -> p b s d", b=2, s=2)

        at_ = [0]

        def take(n):
            at_[0] += n
            return route[:, at_[0] - n:at_[0]]

        def te(v):
            return v.rearrange("p (t e) -> p t e", e=E)

        TE = T * E
        r_s, r_eq, r_cand = take(TE), take(TE), take(TE)
        r_oh1, r_oh2 = take(TE), take(TE)
        r_s2, r_cs, r_in0, r_in1 = take(TE), take(TE), take(TE), take(TE)
        pay = take(TE).rearrange("p (t s c) -> p t s c", s=2, c=4)
        m16 = take(TE // 2).bitcast(F16)
        upper16, ones16 = take(P // 2).bitcast(F16), take(P // 2).bitcast(F16)
        r_max, r_sum, r_v1, r_e1, r_v2, r_e2 = [take(T) for _ in range(6)]
        r_n, r_tiles, r_end, r_base, r_tmp = [take(E) for _ in range(5)]
        assert at_[0] <= 3072 and ET * E <= 3 * TE
        j_a = route[:, 0:ET * E].rearrange("p (j e) -> p j e", e=E)
        j_b = route[:, 5 * TE:5 * TE + ET * E].rearrange("p (j e) -> p j e", e=E)

        ps = ctx.enter_context(nc.psum_tensor("ps", [P, 8, 512], F32))
        def halves(bank, k):
            return ps[:, bank, 0:k * P].bitcast(F16).rearrange("p (a k n) -> p a k n", a=2, k=k)
        p_tx, p_th, p_xa, p_rt = halves(0, KD), halves(1, KD), ps[:, 2, 0:P], ps[:, 3, 0:2 * E]
        p_h = [ps[:, 4, :], ps[:, 5, :]]
        p_cw, p_lat, p_lbt = [ps[:, b, :] for b in (3, 5, 6, 7)], ps[:, 2, :], ps[:, 1, :]
        split_pairs = [(p_lat.rearrange("p (k n) -> p k n", k=KD), lat[:, :, HI, :], lat[:, :, LO, :], 1)] + \
                      [(p_cw[k], cw[:, k, HI, :], cw[:, k, LO, :], 0) for k in range(KD)]
        p_rank, p_count = ps[:, 0, 0:TE], ps[:, 0, TE:2 * TE]
        logits = ps[:, 7, 0:T * E].rearrange("p (t e) -> p t e", e=E)
        p_fth, p_at = halves(0, KD), halves(1, KH)
        p_g = [ps[:, 2, 0:H], ps[:, 3, 0:H]]
        p_u = [ps[:, 4, 0:H], ps[:, 5, 0:H]]
        p_y = [ps[:, 6, :], ps[:, 7, :]]

        def sems(*names):
            return [sem(n) for n in names]

        s_const, s_z = sems("s_const", "s_z")
        s_cw, s_la, s_pin = sems("s_cw", "s_la", "s_pin")
        s_csum, s_pmx = sems("s_csum", "s_pmx")
        s_par, s_pc = sems("s_par", "s_pc")
        s_pt, s_phi, s_plo = sems("s_pt", "s_phi", "s_plo")
        s_meta0 = sem("s_meta0")
        s_xld = sems("s_xld0", "s_xld1")
        s_xmx, s_xex, s_xiv, s_xsc = sems("s_xmx", "s_xex", "s_xiv", "s_xsc")
        s_xhi, s_xlo, s_tx, s_xt = sems("s_xhi", "s_xlo", "s_tx", "s_xt")
        s_xa, s_xam, s_h = sems("s_xa", "s_xam", "s_h")
        s_hmx, s_hex, s_hiv, s_hsc = sems("s_hmx", "s_hex", "s_hiv", "s_hsc")
        s_ch, s_hhi, s_hlo, s_hst = sems("s_ch", "s_hhi", "s_hlo", "s_hst")
        s_th, s_ht = sems("s_th", "s_ht")
        s_rt, s_rlog, s_log = sems("s_rt", "s_rlog", "s_log")
        s_wld = sems("s_wld_gate", "s_wld_up", "s_wld_down")
        s_pad, s_wsum, s_war = sems("s_pad", "s_wsum", "s_war")
        s_wex, s_wiv, s_wsc = sems("s_wex", "s_wiv", "s_wsc")
        s_wss, s_whi, s_wfree = sems("s_wss", "s_whi", "s_wfree")
        s_r, s_rd, s_re, s_m16, s_rmm, s_rcp = sems("s_r", "s_rd", "s_re", "s_m16", "s_rmm", "s_rcp")
        s_pay, s_scat, s_metain, s_et, s_coef = sems("s_pay", "s_scat", "s_metain", "s_et", "s_coef")
        s_hin, s_hgat = sems("s_hin0", "s_hin1"), sems("s_hgat0", "s_hgat1")
        s_ix, s_fth, s_fht = sems("s_ix", "s_fth", "s_fht")
        s_gu, s_silu, s_a = sems("s_gu", "s_silu", "s_a")
        s_amx, s_aex, s_aiv, s_asc, s_cy = sems("s_amx", "s_aex", "s_aiv", "s_asc", "s_cy")
        s_ahi, s_alo, s_ta, s_at, s_dn = sems("s_ahi", "s_alo", "s_ta", "s_at", "s_dn")
        s_y, s_yst = sem("s_y"), sems("s_yst0", "s_yst1")
        s_xin, s_acc, s_pst = sems("s_xin0", "s_xin1"), sem("s_acc"), sems("s_pst0", "s_pst1")
        s_ixl, s_ixe = sems("s_ixl", "s_ixe")
        s_g, s_ge, s_pld = sems("s_g0", "s_g1"), sem("s_ge"), sem("s_pld")
        s_addl, s_adde = sems("s_addl", "s_adde")
        s_out, s_oute = sems("s_out0", "s_out1"), sem("s_oute")

        block = ctx.enter_context(nc.Block())

        def tval(c, i, k=0, per=6):
            return c + k if i is None else c + k + i * per

        def chunk(c, i):
            if c < 3:
                return c % 3, E + 1
            return c % 3, tval(c // 3 - 1, i, 0, 2)

        QN = 3 * EX

        def summed_chunk(c):
            return c if 0 <= c < QN - 1 else QN - 1 if c == QN else None

        def scaled_chunk(c):
            return c - 1 if 0 <= c - 1 < QN - 1 else QN - 1 if c == QN + 1 else None

        class Slot:
            def __init__(s, c, i=None):
                shared = c < N1 or c >= N2
                per = 4 if shared else 2
                s.i = i
                s.c, s.n, s.par = c, tval(c, i, 0, per), c % 2
                s.shared = shared
                if shared:
                    m = c if c < N1 else c - N2
                    tile = m // 2 if c < N1 else S1T + m // 2
                    s.half = m % 2
                    s.hc = m // 2 if c < N1 else H2 + m // 2
                    s.h, s.tile, s.tpar = tval(s.hc, i, 0, 2), tval(tile, i, 0, 2), tile % 2
                    s.tq = tval(tile // 2, i, 0, 1)
                    s.first = c < N1
                    s.expert = E + s.half
                    s.last = s.half == 1
                    s.k = tval(m if c < N1 else c - ET, i, 0, 4)
                else:
                    s.hc = H1 + c - N1
                    s.h, s.j, s.last = tval(s.hc, i, 0, 2), tval(c - N1, i, 0, 2), True
                s.hpar = s.hc % 2

        def run_slots(eng, do, after=None):
            def straight(c):
                do(Slot(c), Slot(c - 1) if c else None)
                if after and c < LEAD:
                    after(c)

            def loop(start, count, per):
                with eng.Fori(0, count) as i:
                    for c in range(start, start + per):
                        prev = Slot(c - 1, i)
                        do(Slot(c, i), prev)
            for start, end, per, lead in ((0, N1, 4, LEAD), (N1, N2, 2, 3), (N2, NS, 4, 3)):
                for c in range(start, start + lead):
                    straight(c)
                count = (end - start - lead - 1) // per
                loop(start + lead, count, per)
                for c in range(start + lead + count * per, end):
                    straight(c)

        def tail(do):
            do(None, Slot(NS - 1))

        def yst_before(s):
            return (s.c - N1) // 2 * 16 if isinstance(s.j, int) else (s.j - (s.c - N1)) * 8 + (s.c - N1) // 2 * 16

        def col(table, n):
            return table[:, n:n + 1] if isinstance(n, int) else table[:, ds(n, 1)]

        def landing(c):
            return stage_down if c % 3 == DOWN and c != QN - 1 else stage[:, c % 3 % 2, :]

        def landed(c, i):
            if c == QN - 1:
                return s_wld[GATE], 16 * EX + 32
            return s_wld[c % 3], tval(c // 3, i, 1, 2) * (32 if c % 3 == DOWN else 16)

        def w_views(c, i, half):
            kind, e = chunk(c, i)
            w = (wg, wu, wd)[kind]
            k, n = (KH, D) if kind == DOWN else (KD, H)
            dst = w[:, e, :, half, :] if isinstance(e, int) else \
                w[:, ds(e, 1), :, half, :].rearrange("p a k n -> p (a k) n")
            return dst, landing(c)[:, 0:k * n].rearrange("p (k n) -> p k n", k=k)

        @block.sync
        def _(sp):
            def load_x(c, i):
                t = tval(c, i)
                if c >= 2:
                    sp.wait_ge(s_xlo, tval(c, i, -1))
                src = x_rows[t] if i is None else x_rows[ds(t, 1)].rearrange("a p d -> (a p) d")
                sp.dma_start(xrow[:, c % 2, :], src).then_inc(s_xld[c % 2], 16)

            w_src = stage[:, :, :].rearrange("p b n -> p (b n)")
            sp.dma_start(w_src[:, KD * D:KD * D + D], lora_a.rearrange("a r d -> (a r) d")).then_inc(s_la, 16)
            sp.dma_start(w_src[:, 0:KD * D].rearrange("p (c d) -> p c d", c=KD),
                         cond_w.rearrange("(c p) d -> p c d", p=P)).then_inc(s_cw, 16)
            sp.dma_start(wr32, w_router.rearrange("(k p) e -> p k e", p=P)).then_inc(s_la, 16)
            load_x(0, None)
            sp.dma_start(pcol[:, 0:1], scalings.unsqueeze(1).broadcast_to([NA, RANK])).then_inc(s_pin, 16)
            sp.dma_start(lmask[:, :].bitcast(I32), adapter_idx.partition_broadcast(P)).then_inc(s_pin, 16)
            for c in range(KD):
                sp.dma_start(
                    w_src[:, KD * D + D + c * P:KD * D + D + (c + 1) * P].rearrange("p (a r) -> p a r", a=NA),
                    lora_b[:, c * P:(c + 1) * P, :].rearrange("a p r -> p a r")).then_inc(s_pin, 16)
            load_x(1, None)

            def load_w(c, i):
                kind, e = chunk(c, i)
                if c == 0:
                    sp.wait_ge(s_pmx, 2)
                    sp.wait_ge(s_csum, 1)
                    sp.wait_ge(s_pt, KD + 2)
                elif c == QN - 1:
                    sp.wait_ge(s_wfree, QN - 2)
                elif c >= 3:
                    sp.wait_ge(s_wfree, tval(c, i, -2))
                if i is None and e >= E:
                    half = e - E
                    src = [ws_gate[:, half * H:(half + 1) * H], ws_up[:, half * H:(half + 1) * H],
                           ws_down[half * H:(half + 1) * H, :]][kind]
                else:
                    src = [we_gate, we_up, we_down][kind]
                    src = src[e] if i is None else src[ds(e, 1)].rearrange("a r n -> (a r) n")
                dst, signal = landing(c), landed(c, i)[0]
                if kind == DOWN:
                    whole = (KH - 1) * P
                    sp.dma_start(dst[:, 0:(KH - 1) * D].rearrange("p (k d) -> p k d", d=D),
                                 src[0:whole, :].rearrange("(k p) d -> p k d", p=P)).then_inc(signal, 16)
                    sp.dma_start(dst[0:HR, (KH - 1) * D:KH * D], src[whole:H, :]).then_inc(signal, 16)
                else:
                    sp.dma_start(dst[:, 0:KD * H].rearrange("p (k h) -> p k h", h=H),
                                 src.rearrange("(k p) h -> p k h", p=P)).then_inc(signal, 16)

            def store_h(c, i):
                t = tval(c, i)
                sp.wait_ge(s_hlo, tval(c, i, 1))
                dst = h_tiles[t] if i is None else h_tiles[ds(t, 1)].rearrange("a p d -> (a p) d")
                sp.dma_start(dst, h16[:, :, :].rearrange("p a d -> p (a d)")).then_inc(s_hst, 16)

            def step(c, i=None):
                if 2 <= c + 3 < T:
                    load_x(c + 3, i)
                if 0 <= c - 1 < T:
                    store_h(c - 1, i)
                if 0 <= c + 1 < QN - 1:
                    load_w(c + 1, i)
                if c == QN - 1:
                    load_w(QN - 1, i)

            for c in range(-1, 2):
                step(c)
            with sp.Fori(0, 4) as i:
                for c in range(2, 8):
                    step(c, i)
            for c in range(26, T - 1):
                step(c)


            def load_h(s):
                if s.c >= 2 * 2 or not s.first:
                    sp.wait_ge(s_fth, s.h - 1)
                src = h_tiles[s.tile] if isinstance(s.tile, int) else h_tiles[ds(s.tile, 1)].rearrange("a p d -> (a p) d")
                sp.dma_start(hin[:, s.hpar, :, :].rearrange("p a d -> p (a d)"), src).then_inc(s_hin[s.hpar], 16)

            def load_acc(s):
                if s.first and s.c >= 4:
                    sp.wait_ge(s_pst[s.tpar], s.tq * 16)
                elif not s.first:
                    if s.c < N2 + 4:
                        sp.wait_ge(s_pst[s.tpar], s.tq * 16)
                    else:
                        sp.wait_ge(s_out[s.tpar], (s.tq - S1T // 2 - (s.tpar == 0)) * 16)
                src = x_rows[s.tile] if isinstance(s.tile, int) else x_rows[ds(s.tile, 1)].rearrange("a p d -> (a p) d")
                sp.dma_start(acc[:, s.tpar, :], src).then_inc(s_xin[s.tpar], 16)

            def store_part(s):
                sp.wait_ge(s_acc, s.k + 1)
                dst = part_tiles[s.tile] if isinstance(s.tile, int) else part_tiles[ds(s.tile, 1)].rearrange("a p d -> (a p) d")
                sp.dma_start(dst, acc[:, s.tpar, :]).then_inc(s_pst[s.tpar], 16)

            def store_y(s):
                sp.wait_ge(s_y, s.j + 1)
                dst = y_tiles[s.j] if isinstance(s.j, int) else y_tiles[ds(s.j, 1)].rearrange("a p d -> (a p) d")
                sp.dma_start(dst, yout[:, s.par, :]).then_inc(s_yst[s.par], 16)

            sp.wait_ge(s_wfree, QN - 1)
            sp.wait_ge(s_hst, 16 * 2)
            for t in range(2):
                load_h(Slot(2 * t))
            step(T - 1)
            step(T)
            sp.wait_ge(s_rt, T)
            for t in range(2):
                load_acc(Slot(2 * t))
            load_h(Slot(4))
            store_part(Slot(1))
            load_acc(Slot(4))
            with sp.Fori(0, (S1T - 3) // 2) as i:
                for t in range(1, 3):
                    load_h(Slot(2 * t + 4, i))
                    store_part(Slot(2 * t + 1, i))
                    load_acc(Slot(2 * t + 4, i))
            for t in range(S1T - 2, S1T):
                store_part(Slot(2 * t + 1))
            with sp.Fori(0, (ET - 3) // 2) as i:
                for c in range(N1, N1 + 2):
                    store_y(Slot(c, i))
            load_h(Slot(N2))
            load_acc(Slot(N2))
            store_y(Slot(N2 - 3))
            load_h(Slot(N2 + 2))
            load_acc(Slot(N2 + 2))
            store_y(Slot(N2 - 2))
            store_y(Slot(N2 - 1))
            load_h(Slot(N2 + 4))
            with sp.Fori(0, (T - S1T - 3) // 2) as i:
                for c in (N2 + 6, N2 + 8):
                    load_h(Slot(c, i))
                    load_acc(Slot(c - 2, i))
            load_acc(Slot(NS - 2))

        @block.gpsimd
        def _(pool):
            pool.memset(ident, 0.0).then_inc(s_z, 1)
            pool.wait_ge(s_z, 1)
            pool.affine_select(out=ident, in_=ident, compare_op=ALU.not_equal, fill=1.0, base=0,
                               pattern=[[-1, P]], channel_multiplier=1).then_inc(s_const, 1)
            pool.memset(scale_c[:, 0:1], float((254 + TOP) * ONE_EXP)).then_inc(s_const, 1)
            pool.memset(scale_c[:, 1:2], float((254 + TOP - MIN_EXP) * ONE_EXP)).then_inc(s_const, 1)
            pool.wait_ge(s_const, 3)
            pool.tensor_copy(ident16[:, :], ident).then_inc(s_const, 1)
            pool.iota(iota_e[:, :], [[1, E]], base=0, channel_multiplier=0,
                      allow_small_or_imprecise_dtypes=True).then_inc(s_const, 1)
            pool.iota(iota_j[:, :], [[1, ET]], base=0, channel_multiplier=0,
                      allow_small_or_imprecise_dtypes=True).then_inc(s_const, 1)
            pool.iota(pcol[:, 1:2].bitcast(I32), [[0, 1]], base=0, channel_multiplier=1).then_inc(s_const, 1)
            zeros = x16[:, :, :].rearrange("p a d -> p (a d)").bitcast(F32)[:, 0:SLOTS * 4 // P]
            pool.memset(zeros, 0.0).then_inc(s_z, 1)
            pool.wait_ge(s_z, 2)
            pool.dma_start(meta_dram.rearrange("(p j) c -> p (j c)", p=P), zeros).then_inc(s_meta0, 16)
            pool.memset(stage_down[HR:P, (KH - 1) * D:KH * D], 0.0).then_inc(s_pad, 1)
            pool.wait_ge(s_pad, 1)
            pool.wait_ge(s_pmx, 2)
            pool.wait_ge(s_csum, 1)
            pool.partition_all_reduce(rexp[:, 0, 0:3], small[:, 8:11], P, bass.bass_isa.ReduceOp.max).then_inc(s_par, 1)


            def maximum(c, i):
                pool.wait_ge(s_wsum, tval(c, i, 1))
                pool.nop(nofuse=True)
                b = c % 2
                pool.partition_all_reduce(small[:, 14 + b:15 + b], small[:, 12 + b:13 + b], P,
                                          bass.bass_isa.ReduceOp.max).then_inc(s_war, 1)

            def low(c, i):
                hi, src = w_views(c, i, HI)
                lo, _ = w_views(c, i, LO)
                pool.wait_ge(s_whi, tval(c, i, 1))
                pool.nop(nofuse=True)
                pool.tensor_tensor(lo, src, hi, ALU.subtract).then_inc(s_wfree, 1)

            def step(c, i=None):
                if c + 1 < QN - 1:
                    maximum(c + 1, i)
                low(c, i)
                if c + 1 == QN - 1:
                    maximum(c + 1, i)
                if c == QN - 3:
                    pool.wait_ge(s_wfree, QN - 2)
                    pool.memset(stage[HR:P, 0, (KH - 1) * D:KH * D], 0.0).then_inc(s_pad, 1)
                    pool.wait_ge(s_pad, 2)

            maximum(0, None)
            for c in range(0, 3):
                step(c)
            with pool.Fori(0, 4) as i:
                for c in range(3, 9):
                    step(c, i)
            for c in range(QN - 3, QN):
                step(c)

            pool.wait_ge(s_h, T)
            pool.memset(ones16, 1.0).then_inc(s_z, 1)
            pool.wait_ge(s_z, 3)
            pool.affine_select(out=upper16, in_=ones16, compare_op=ALU.is_gt, fill=0.0, base=0,
                               pattern=[[1, P]], channel_multiplier=-1).then_inc(s_const, 1)
            pool.iota(pay[:, :, :, 0].bitcast(I32), [[P, T], [0, 2]], base=0, channel_multiplier=1).then_inc(s_const, 1)
            pool.memset(pay[:, :, :, 3], 0.0).then_inc(s_const, 1)
            pool.wait_ge(s_meta0, 16)
            pool.wait_ge(s_const, 10)
            pool.wait_ge(s_pay, 2)
            for t in range(T):
                for k in range(2):
                    pool.indirect_dma_start(
                        out=meta_dram, out_offset=bass.IndirectOffsetOnAxis(ap=pos[:, t, k:k + 1], axis=0),
                        in_=pay[:, t, k, :], in_offset=None).then_inc(s_scat, 16)
            pool.wait_ge(s_scat, 16 * 2 * T)
            pool.dma_start(meta[:, :, :], meta_dram[0:ET * P, :].rearrange("(j p) c -> p j c", p=P)).then_inc(s_metain, 16)
            pool.wait_ge(s_metain, 16)
            pool.wait_ge(s_hst, 16 * T)

            def gather_h(s):
                pool.wait_ge(s_fth, s.h - 1)
                col = meta[:, s.j, 0:1] if isinstance(s.j, int) else \
                    meta[:, ds(s.j, 1), 0:1].rearrange("p a c -> p (a c)")
                pool.tensor_copy(idx[:, s.hpar:s.hpar + 1], col.bitcast(I32)).then_inc(s_ix, 1)
                pool.wait_ge(s_ix, s.j + 1)
                pool.nop(nofuse=True)
                pool.indirect_dma_start(
                    out=hin[:, s.hpar, :, :].rearrange("p a d -> p (a d)"), out_offset=None, in_=h_dram,
                    in_offset=bass.IndirectOffsetOnAxis(ap=idx[:, s.hpar:s.hpar + 1], axis=0)
                ).then_inc(s_hgat[s.hpar], 16)

            gather_h(Slot(N1))
            with pool.Fori(0, (ET - 1) // 2) as i:
                for c in range(N1 + 1, N1 + 3):
                    gather_h(Slot(c, i))

            pool.wait_ge(s_yst[0], 16 * ((ET + 1) // 2))
            pool.wait_ge(s_yst[1], 16 * (ET // 2))

            def rows_of(t, gathered, cols, i, s_idx, before, landed):
                for k in range(2):
                    col_ = pos[:, t, k:k + 1] if i is None else \
                        pos[:, ds(t, 1), k:k + 1].rearrange("p a c -> p (a c)")
                    pool.tensor_copy(posb[:, cols + k:cols + k + 1], col_).then_inc(s_idx, 1)
                pool.wait_ge(s_idx, 2 + 2 * before)
                pool.nop(nofuse=True)
                for k in range(2):
                    pool.indirect_dma_start(
                        out=gathered[k], out_offset=None, in_=y_dram,
                        in_offset=bass.IndirectOffsetOnAxis(ap=posb[:, cols + k:cols + k + 1], axis=0)
                    ).then_inc(landed, 16)

            def add_rows(t, total, s_total, count, gathered, i, s_sum, before, stored):
                pool.tensor_tensor(gathered[0], gathered[0], gathered[1], ALU.add).then_inc(s_sum, 1)
                pool.wait_ge(s_sum, 1 + 2 * before)
                pool.wait_ge(s_total, count)
                pool.tensor_tensor(total, total, gathered[0], ALU.add).then_inc(s_sum, 1)
                pool.wait_ge(s_sum, 2 + 2 * before)
                pool.nop(nofuse=True)
                dst = out_rows[t] if i is None else out_rows[ds(t, 1)].rearrange("a p d -> (a p) d")
                pool.dma_start(dst, total).then_inc(stored, 16)

            def fetch_late(k, i=None):
                b = (S1T + k) % 2
                rows_of(tval(S1T + k, i, 0, 2), [gat[:, b, 0, :], gat[:, b, 1, :]], 2 * b, i, s_ixl,
                        tval(k, i, 0, 2), s_g[b])

            def sum_late(k, i=None):
                b = (S1T + k) % 2
                pool.wait_ge(s_g[b], tval(k // 2, i, 1, 1) * 32)
                add_rows(tval(S1T + k, i, 0, 2), acc[:, b, :], s_acc, 2 + 2 * tval(S1T + k, i, 0, 2), [gat[:, b, 0, :], gat[:, b, 1, :]], i, s_addl,
                         tval(k, i, 0, 2), s_out[b])

            def fetch_early(k, i=None):
                t = tval(k, i, 0, 1)
                if k:
                    pool.wait_ge(s_oute, t * 16)
                    pool.nop(nofuse=True)
                src = part_tiles[t] if i is None else part_tiles[ds(t, 1)].rearrange("a p d -> (a p) d")
                pool.dma_start(part[:, :], src).then_inc(s_pld, 16)
                rows_of(t, [yout[:, 0, :], yout[:, 1, :]], 4, i, s_ixe, t, s_ge)

            def sum_early(k, i=None):
                t = tval(k, i, 0, 1)
                pool.wait_ge(s_ge, 32 * tval(k, i, 1, 1))
                add_rows(t, part[:, :], s_pld, 16 * tval(k, i, 1, 1), [yout[:, 0, :], yout[:, 1, :]], i, s_adde, t, s_oute)

            def round_(i, early):
                fetch_late(1, i)
                if early:
                    fetch_early(1, i)
                sum_late(0, i)
                fetch_late(2, i)
                if early:
                    sum_early(1, i)
                sum_late(1, i)

            rounds = (T - S1T - 1) // 2
            pool.wait_ge(s_pst[0], 16 * ((S1T + 1) // 2))
            pool.wait_ge(s_pst[1], 16 * (S1T // 2))
            fetch_early(0)
            fetch_late(0)
            sum_early(0)
            with pool.Fori(0, S1T - 1) as i:
                round_(i, True)
            if rounds > S1T - 1:
                with pool.Fori(S1T - 1, rounds) as i:
                    round_(i, False)
            sum_late(T - S1T - 1)
            pool.wait_ge(s_out[0], 16 * (T // 2 - (S1T + 1) // 2))
            pool.wait_ge(s_out[1], 16 * (T // 2 - S1T // 2))
            pool.wait_ge(s_oute, 16 * S1T)

        @block.scalar
        def _(a):
            def sum_w(c, i):
                signal, count = landed(c, i)
                a.wait_ge(signal, count)
                if c % 3 == DOWN:
                    a.wait_ge(s_pad, 2 if c == QN - 1 else 1)
                if c == QN - 1:
                    a.wait_ge(s_wfree, QN - 3)
                a.nop(nofuse=True)
                dst, src = w_views(c, i, HI)
                nc.scalar.activation(dst, src, ACT.Abs,
                                     accum_out=small[:, 12 + c % 2:13 + c % 2]).then_inc(s_wsum, 1)

            def split_w(c, i):
                a.wait_ge(s_wss, tval(c, i, 1))
                a.nop(nofuse=True)
                dst, src = w_views(c, i, HI)
                nc.scalar.activation(dst, src, ACT.Copy).then_inc(s_whi, 1)

            def copy_ht(h, hpar):
                a.wait_ge(s_fth, h + 1)
                nc.scalar.activation(ht[hpar], p_fth, ACT.Copy).then_inc(s_fht, 1)

            def copy_xt(c, i):
                a.wait_ge(s_tx, tval(c, i, 2))
                if c >= 2:
                    a.wait_ge(s_rt, tval(c, i, -1))
                nc.scalar.activation(xt[:, (c + 1) % 2, :, :, :], p_tx, ACT.Copy).then_inc(s_xt, 1)

            def step(c, i=None):
                t = tval(c, i)
                if 0 <= c + 1 < T:
                    copy_xt(c, i)
                if 0 <= c + 2 < T:
                    a.wait_ge(s_xsc, tval(c, i, 3))
                    if c == -2:
                        a.wait_ge(s_meta0, 16)
                    nc.scalar.activation(x16[:, HI, :], xrow[:, c % 2, :], ACT.Copy,
                                         scale=small[:, 2 + c % 2:3 + c % 2]).then_inc(s_xhi, 1)
                if summed_chunk(c) is not None:
                    sum_w(summed_chunk(c), i)
                if c == T - 1:
                    a.wait_ge(s_wfree, QN - 1)
                    copy_ht(0, 0)
                if 0 <= c - 1 < T:
                    a.wait_ge(s_th, tval(c, i))
                    nc.scalar.activation(xt[:, c % 2, :, :, :], p_th, ACT.Copy).then_inc(s_ht, 1)
                if scaled_chunk(c) is not None:
                    split_w(scaled_chunk(c), i)
                if 0 <= c < T:
                    a.wait_ge(s_hsc, tval(c, i, 1))
                    if c >= 1:
                        a.wait_ge(s_hst, tval(c, i) * 16)
                    nc.scalar.activation(h16[:, HI, :], p_h[c % 2], ACT.Copy, scale=small[:, 7:8]).then_inc(s_hhi, 1)

            a.wait_ge(s_cw, 16)
            w_src = stage[:, :, :].rearrange("p b n -> p (b n)")
            nc.scalar.activation(cw[:, :, HI, :], w_src[:, 0:KD * D].rearrange("p (k d) -> p k d", k=KD), ACT.Abs,
                                 accum_out=small[:, 8:9]).then_inc(s_csum, 1)
            step(-2)
            step(-1)
            a.wait_ge(s_pc, 2)
            for k, (bank, hi, _, part) in enumerate(split_pairs):
                a.wait_ge(s_pt, KD + 1 if part else k)
                nc.scalar.activation(hi, bank, ACT.Copy, scale=rexp[:, 2, part:part + 1]).then_inc(s_phi, 1)
            a.wait_ge(s_pt, KD + 2)
            nc.scalar.activation(lbt[:, :], p_lbt, ACT.Copy).then_inc(s_phi, 1)
            nc.scalar.activation(wr[:, :, HI, :], wr32, ACT.Copy, scale=rexp[:, 2, 2:3]).then_inc(s_phi, 1)

            for c in range(0, 4):
                step(c)
            with a.Fori(0, 4) as i:
                for c in range(4, 10):
                    step(c, i)
            for c in range(28, T):
                step(c)
            step(T)

            def beside(c):
                if c == 0:
                    a.wait_ge(s_rd, 1)
                    nc.scalar.activation(r_s, r_s, ACT.Exp).then_inc(s_re, 1)

            def slot(s, prev):
                if s and s.last and s.c < NS - 1:
                    copy_ht(s.h + 1, 1 - s.hpar)
                if prev:
                    a.wait_ge(s_ta, prev.n + 1)
                    nc.scalar.activation(at[:, prev.par, :, :, :], p_at, ACT.Copy).then_inc(s_at, 1)
                if s:
                    a.wait_ge(s_gu, s.n + 1)
                    if s.c == 0:
                        a.wait_ge(s_coef, 12)
                    if s.c == N1:
                        a.wait_ge(s_coef, 15)
                    nc.scalar.activation(act[:, :], p_g[s.par], ACT.Silu, scale=col(cg, s.n)).then_inc(s_silu, 1)
                    a.wait_ge(s_asc, s.n + 1)
                    nc.scalar.activation(a16[:, HI, :], act[:, :], ACT.Copy, scale=fsm[:, 2:3]).then_inc(s_ahi, 1)
                if prev and not prev.shared:
                    a.wait_ge(s_dn, prev.n + 1)
                    a.wait_ge(s_cy, prev.n + 1)
                    if prev.c >= N1 + 2:
                        a.wait_ge(s_yst[prev.par], yst_before(prev))
                    nc.scalar.activation(yout[:, prev.par, :], p_y[prev.par], ACT.Copy,
                                         scale=col(cy, prev.n)).then_inc(s_y, 1)

            a.wait_ge(s_wfree, QN)
            run_slots(a, slot, beside)
            tail(slot)

        @block.vector
        def _(v):
            V = nc.vector

            def row_max(o, src, axis=AX):
                return V.tensor_reduce(o, src, axis, ALU.max, apply_absolute_value=True)

            def exponent(o, amax):
                return V.tensor_scalar(o.bitcast(I32), amax.bitcast(I32), EXP_MASK, None, ALU.bitwise_and)

            def inverse(o, ex):
                return V.tensor_scalar(o.bitcast(I32), ex.bitcast(I32), float(MIN_EXP * ONE_EXP),
                                       float(-TOP * ONE_EXP), ALU.max, ALU.add)

            def scale_of(o, inv):
                return V.tensor_scalar(o.bitcast(I32), inv.bitcast(I32), -1.0, float(254 * ONE_EXP),
                                       ALU.mult, ALU.add)

            def scale_from(o, ex):
                return V.scalar_tensor_tensor(out=o.bitcast(I32), in0=scale_c[:, 0:1], scalar=ex.bitcast(I32),
                                              in1=scale_c[:, 1:2], op0=ALU.subtract, op1=ALU.min)

            def scale_xa(c, i):
                v.wait_ge(s_xa, tval(c, i, 1))
                V.tensor_scalar(xam[:, :], p_xa, col(lmask, tval(c // 2, i, 0, 3)), None,
                                ALU.mult).then_inc(s_xam, 1)

            def max_x(c, i):
                v.wait_ge(s_xld[(c + 1) % 2], tval((c + 3) // 2, i, 1, 3) * 16)
                row_max(small[:, 0:1], xrow[:, (c + 1) % 2, :]).then_inc(s_xmx, 1)

            def exponent_x(c, i):
                v.wait_ge(s_xmx, tval(c, i, 4))
                exponent(small[:, 1:2], small[:, 0:1]).then_inc(s_xex, 1)

            def scale_x(c, i):
                v.wait_ge(s_xex, tval(c, i, 4))
                b = (c + 1) % 2
                scale_from(small[:, 2 + b:3 + b], small[:, 1:2]).then_inc(s_xsc, 1)
                inverse(col(xinv, tval(c, i, 3)), small[:, 1:2]).then_inc(s_xiv, 1)

            def step(c, i=None):
                def tab(table, k):
                    n = tval(c, i, k)
                    return col(table, n)
                x_ = 0 <= c + 2 < T
                q = scaled_chunk(c)
                w_ = q is not None
                if x_:
                    nx = tval(c, i, 3)
                if w_:
                    kind, e = chunk(q, i)
                    nw = tval(q, i, 1)
                    v.wait_ge(s_war, nw)
                    exponent(small[:, 8:9], small[:, 14 + q % 2:15 + q % 2]).then_inc(s_wex, 1)
                if 0 <= c < T:
                    scale_xa(c, i)
                if w_:
                    v.wait_ge(s_wex, nw)
                    scale_from(small[:, 9:10], small[:, 8:9]).then_inc(s_wsc, 1)
                    inv = winv[:, kind, e:e + 1] if isinstance(e, int) else winv[:, kind, ds(e, 1)]
                    inverse(inv, small[:, 8:9]).then_inc(s_wiv, 1)
                    v.wait_ge(s_wsc, nw)
                    _, src = w_views(q, i, HI)
                    V.tensor_scalar(src, src, small[:, 9:10], None, ALU.mult).then_inc(s_wss, 1)
                if x_:
                    v.wait_ge(s_xhi, nx)
                    V.scalar_tensor_tensor(out=x16[:, LO, :], in0=xrow[:, c % 2, :],
                                           scalar=small[:, 2 + c % 2:3 + c % 2], in1=x16[:, HI, :],
                                           op0=ALU.mult, op1=ALU.subtract).then_inc(s_xlo, 1)
                if 0 <= c < T:
                    n = tval(c, i, 1)
                    v.wait_ge(s_h, n)
                    row_max(small[:, 4:5], p_h[c % 2]).then_inc(s_hmx, 1)
                if 0 <= c < T:
                    v.wait_ge(s_hmx, n)
                    exponent(small[:, 5:6], small[:, 4:5]).then_inc(s_hex, 1)
                    v.wait_ge(s_hex, n)
                    scale_from(small[:, 7:8], small[:, 5:6]).then_inc(s_hsc, 1)
                    inverse(small[:, 6:7], small[:, 5:6]).then_inc(s_hiv, 1)
                if 0 <= c - 2 < T:
                    v.wait_ge(s_rt, tval(c, i, -1))
                    if c >= 3:
                        v.wait_ge(s_log, tval(c, i, -2))
                    V.tensor_scalar(rlog[:, :, :].rearrange("p a e -> p (a e)"), p_rt, tab(ch, -2), rexp[:, 1, 2:3],
                                    ALU.mult, ALU.mult).then_inc(s_rlog, 1)
                if 0 <= c + 3 < T:
                    max_x(c, i)
                if 0 <= c - 2 < T:
                    v.wait_ge(s_rlog, tval(c, i, -1))
                    t2 = tval(c, i, -2)
                    dst = logits[:, t2, :] if i is None else logits[:, ds(t2, 1), :].rearrange("p a e -> p (a e)")
                    V.tensor_tensor(dst, rlog[:, 0, :], rlog[:, 1, :], ALU.add).then_inc(s_log, 1)
                if 0 <= c + 3 < T:
                    exponent_x(c, i)
                if 0 <= c < T:
                    v.wait_ge(s_hiv, n)
                    v.wait_ge(s_xiv, n)
                    V.tensor_scalar(tab(ch, 0), small[:, 6:7], tab(xinv, 0), rexp[:, 1, 0:1],
                                    ALU.mult, ALU.mult).then_inc(s_ch, 1)
                if 0 <= c + 3 < T:
                    scale_x(c, i)
                if 0 <= c < T:
                    v.wait_ge(s_hhi, n)
                    V.scalar_tensor_tensor(out=h16[:, LO, :], in0=p_h[c % 2], scalar=small[:, 7:8],
                                           in1=h16[:, HI, :], op0=ALU.mult, op1=ALU.subtract).then_inc(s_hlo, 1)
                    v.wait_ge(s_ch, n)

            w_src = stage[:, :, :].rearrange("p b n -> p (b n)")
            v.wait_ge(s_la, 16 * 2)
            row_max(small[:, 9:10], w_src[:, KD * D:KD * D + D]).then_inc(s_pmx, 1)
            row_max(small[:, 10:11], early[:, P:P + KD * E]).then_inc(s_pmx, 1)
            max_x(-3, None)
            v.wait_ge(s_const, 7)
            exponent_x(-3, None)
            scale_x(-3, None)
            step(-2)
            v.wait_ge(s_par, 1)
            exponent(rexp[:, 1, 0:3], rexp[:, 0, 0:3]).then_inc(s_plo, 1)
            v.wait_ge(s_plo, 1)
            inverse(rexp[:, 1, 0:3], rexp[:, 1, 0:3]).then_inc(s_pc, 1)
            v.wait_ge(s_pc, 1)
            scale_of(rexp[:, 2, 0:3], rexp[:, 1, 0:3]).then_inc(s_pc, 1)
            v.wait_ge(s_pin, 16 * (2 + KD))
            V.tensor_scalar(pcol[:, 1:2].bitcast(I32), pcol[:, 1:2].bitcast(I32), RANK.bit_length() - 1, None,
                            ALU.arith_shift_right).then_inc(s_pc, 1)
            V.tensor_copy(lmask[:, :], lmask[:, :].bitcast(I32)).then_inc(s_pc, 1)
            v.wait_ge(s_pc, 4)
            V.tensor_copy(pcol[:, 2:3], pcol[:, 1:2].bitcast(I32)).then_inc(s_pc, 1)
            V.tensor_scalar(pcol[:, 3:4], pcol[:, 0:1], rexp[:, 2, 0:1], rexp[:, 1, 1:2],
                            ALU.mult, ALU.mult).then_inc(s_pc, 1)
            v.wait_ge(s_pc, 6)
            V.tensor_scalar(lmask[:, :], lmask[:, :], pcol[:, 2:3], pcol[:, 3:4],
                            ALU.is_equal, ALU.mult).then_inc(s_pc, 1)
            step(-1)
            for k, (bank, hi, lo, part) in enumerate(split_pairs):
                v.wait_ge(s_phi, k + 1)
                V.scalar_tensor_tensor(out=lo, in0=bank, scalar=rexp[:, 2, part:part + 1], in1=hi,
                                       op0=ALU.mult, op1=ALU.subtract).then_inc(s_plo, 1)
            v.wait_ge(s_phi, KD + 3)
            V.scalar_tensor_tensor(out=wr[:, :, LO, :], in0=wr32, scalar=rexp[:, 2, 2:3],
                                   in1=wr[:, :, HI, :], op0=ALU.mult, op1=ALU.subtract).then_inc(s_plo, 1)

            for c in range(0, 4):
                step(c)
            with v.Fori(0, 4) as i:
                for c in range(4, 10):
                    step(c, i)
            for c in range(28, T + 1):
                step(c)

            chain = [0]

            def link(ins):
                chain[0] += 1
                ins.then_inc(s_r, 1)
                v.wait_ge(s_r, chain[0])

            def put(ins):
                chain[0] += 1
                ins.then_inc(s_r, 1)

            def prefix_sums(src, dst, other, unit, n):
                d_ = unit
                while d_ < n:
                    put(V.tensor_copy(dst[:, 0:d_], src[:, 0:d_]))
                    link(V.tensor_tensor(dst[:, d_:n], src[:, d_:n], src[:, 0:n - d_], ALU.add))
                    src, dst, other = dst, other, dst
                    d_ *= 2
                return src, dst

            def by_t(a_):
                return a_.unsqueeze(2).broadcast_to([P, T, E])

            def by_e(a_, n=T):
                return a_.unsqueeze(1).broadcast_to([P, n, E])

            for half in range(2):
                for base, t0, t1 in ((0, 0, S1T), (ET, S1T, T)):
                    for table, kind in ((cg, GATE), (cu, UP), (cd, DOWN)):
                        sel = table[:, base + 2 * t0:base + 2 * t1].rearrange("p (t s) -> p t s", s=2)[:, :, half]
                        w_ = winv[:, kind, E + half:E + half + 1]
                        if kind == DOWN:
                            V.tensor_copy(sel, w_.broadcast_to([P, t1 - t0])).then_inc(s_coef, 1)
                        else:
                            V.tensor_scalar(sel, ch[:, t0:t1], w_, None, ALU.mult).then_inc(s_coef, 1)
            v.wait_ge(s_coef, 12)

            def pick(scores, value, lowest, onehot):
                link(V.tensor_reduce(value, te(scores), AX, ALU.max))
                link(V.tensor_tensor(te(r_eq), te(scores), by_t(value), ALU.is_equal))
                link(V.scalar_tensor_tensor(out=te(r_cand), in0=te(r_eq), scalar=float(-E), in1=by_e(iota_e[:, :]),
                                            op0=ALU.mult, op1=ALU.add))
                link(V.tensor_reduce(lowest, te(r_cand), AX, ALU.min))
                link(V.tensor_tensor(te(onehot), te(r_cand), by_t(lowest), ALU.is_equal))


            totals = []

            def route_scores():
                v.wait_ge(s_re, 1)
                link(V.tensor_reduce(r_sum, te(r_s), AX, ALU.add))
                link(V.reciprocal(r_sum, r_sum))
                link(V.tensor_tensor(te(r_s), te(r_s), by_t(r_sum), ALU.mult))

            def route_first():
                pick(r_s, r_v1, r_e1, r_oh1)

            def route_second():
                link(V.scalar_tensor_tensor(out=r_s2, in0=r_oh1, scalar=-2.0, in1=r_s, op0=ALU.mult, op1=ALU.add))
                pick(r_s2, r_v2, r_e2, r_oh2)
                V.tensor_tensor(m16, r_oh1, r_oh2, ALU.add).then_inc(s_m16, 1)
                v.wait_ge(s_const, 10)
                for k, val in ((0, r_v1), (1, r_v2)):
                    put(V.tensor_copy(pay[:, :, k, 1], ch[:, :]))
                    put(V.tensor_copy(pay[:, :, k, 2], val))

            def route_counts():
                v.wait_ge(s_rmm, 1)
                V.tensor_copy(r_cs, p_count).then_inc(s_rcp, 1)
                V.tensor_copy(r_cand, p_rank).then_inc(s_rcp, 1)
                v.wait_ge(s_rcp, 2)
                put(V.tensor_tensor(r_cand, r_cand, r_cs, ALU.subtract))
                totals.append(prefix_sums(r_cs, r_in0, r_in1, E, TE))

            def route_bases():
                src, dst = totals[0]
                link(V.tensor_scalar(r_tmp.bitcast(I32), src[:, TE - E:TE], float(P - 1), None, ALU.add))
                link(V.tensor_scalar(r_tmp.bitcast(I32), r_tmp.bitcast(I32), P.bit_length() - 1, None,
                                     ALU.arith_shift_right))
                put(V.tensor_scalar(r_tiles, r_tmp.bitcast(I32), float(P), None, ALU.mult))
                link(V.tensor_copy(r_n, r_tmp.bitcast(I32)))
                prefix_sums(r_n, r_end, r_n, 1, E)
                link(V.scalar_tensor_tensor(out=r_base, in0=r_end, scalar=float(P), in1=r_tiles,
                                            op0=ALU.mult, op1=ALU.subtract))

            def route_places():
                src, dst = totals[0]
                link(V.tensor_tensor(dst, src, r_cand, ALU.add))
                link(V.tensor_tensor(te(dst), te(dst), by_e(r_base), ALU.add))
                put(V.tensor_tensor(r_eq, r_oh1, dst, ALU.mult))
                link(V.tensor_tensor(r_cand, r_oh2, dst, ALU.mult))
                put(V.tensor_reduce(r_e1, te(r_eq), AX, ALU.add))
                link(V.tensor_reduce(r_e2, te(r_cand), AX, ALU.add))
                V.tensor_copy(pos[:, :, 0], r_e1).then_inc(s_pay, 1)
                V.tensor_copy(pos[:, :, 1], r_e2).then_inc(s_pay, 1)

            ej = [P, ET, E]

            def route_tiles():
                link(V.tensor_tensor(j_a, iota_j[:, :].unsqueeze(2).broadcast_to(ej), r_end.unsqueeze(1).broadcast_to(ej),
                                     ALU.is_ge))
                link(V.tensor_reduce(r_in1[:, 0:ET], j_a, AX, ALU.add))
                link(V.tensor_scalar(r_in1[:, 0:ET], r_in1[:, 0:ET], float(E - 1), None, ALU.min))
                V.tensor_copy(etile[:, :], r_in1[:, 0:ET]).then_inc(s_et, 1)
                link(V.tensor_tensor(j_a, iota_e[:, :].unsqueeze(1).broadcast_to(ej), r_in1[:, 0:ET].unsqueeze(2).broadcast_to(ej),
                                     ALU.is_equal))

            def tile_coefs(table, kind):
                link(V.tensor_tensor(j_b, j_a, winv[:, kind, 0:E].unsqueeze(1).broadcast_to(ej), ALU.mult))
                link(V.tensor_reduce(table[:, N1:N2], j_b, AX, ALU.add))

            def beside(c):
                if c == 0:
                    route_scores()
                    route_first()
                if c == 1:
                    route_second()
                if c == 3:
                    route_counts()
                    route_bases()
                if c == 4:
                    route_places()
                if c == 5:
                    route_tiles()
                if c == 6:
                    tile_coefs(cg, GATE)
                    tile_coefs(cu, UP)
                if c == 7:
                    tile_coefs(cd, DOWN)

            def slot(s, prev):
                if s and s.c == N1:
                    v.wait_ge(s_metain, 16)
                    for table, k in ((cg, 1), (cu, 1), (cd, 2)):
                        V.tensor_tensor(table[:, N1:N2], table[:, N1:N2], meta[:, :, k], ALU.mult).then_inc(s_coef, 1)
                    v.wait_ge(s_coef, 15)
                if s:
                    n = s.n + 1
                    v.wait_ge(s_silu, n)
                    V.scalar_tensor_tensor(out=act[:, :], in0=p_u[s.par], scalar=col(cu, s.n), in1=act[:, :],
                                           op0=ALU.mult, op1=ALU.mult).then_inc(s_a, 1)
                    v.wait_ge(s_a, n)
                    row_max(fsm[:, 0:1], act[:, :]).then_inc(s_amx, 1)
                    v.wait_ge(s_amx, n)
                    exponent(fsm[:, 0:1], fsm[:, 0:1]).then_inc(s_aex, 1)
                    v.wait_ge(s_aex, n)
                    scale_from(fsm[:, 2:3], fsm[:, 0:1]).then_inc(s_asc, 1)
                    inverse(fsm[:, 1:2], fsm[:, 0:1]).then_inc(s_aiv, 1)
                    v.wait_ge(s_aiv, n)
                    V.tensor_tensor(col(cy, s.n), fsm[:, 1:2], col(cd, s.n), ALU.mult).then_inc(s_cy, 1)
                    v.wait_ge(s_ahi, n)
                    V.scalar_tensor_tensor(out=a16[:, LO, :], in0=act[:, :], scalar=fsm[:, 2:3], in1=a16[:, HI, :],
                                           op0=ALU.mult, op1=ALU.subtract).then_inc(s_alo, 1)
                if prev and prev.shared:
                    v.wait_ge(s_dn, prev.n + 1)
                    v.wait_ge(s_cy, prev.n + 1)
                    if prev.half == 0:
                        v.wait_ge(s_xin[prev.tpar], 16 * (prev.tq + 1))
                    else:
                        v.wait_ge(s_acc, prev.k)
                    V.scalar_tensor_tensor(out=acc[:, prev.tpar, :], in0=p_y[prev.par], scalar=col(cy, prev.n),
                                           in1=acc[:, prev.tpar, :], op0=ALU.mult, op1=ALU.add).then_inc(s_acc, 1)

            step(T + 1)
            v.wait_ge(s_log, T)
            link(V.tensor_reduce(r_max, logits[:, :, :], AX, ALU.max))
            V.tensor_tensor(te(r_s), logits[:, :, :], by_t(r_max), ALU.subtract).then_inc(s_rd, 1)
            run_slots(v, slot, beside)
            tail(slot)

        @block.tensor
        def _(pe):
            w_src = stage[:, :, :].rearrange("p b n -> p (b n)")
            pe.wait_ge(s_cw, 16)
            pe.wait_ge(s_const, 1)
            for k in range(KD):
                for c in range(KD):
                    mm = pe.transpose(p_cw[k][:, c * P:(c + 1) * P], w_src[:, c * D + k * P:c * D + (k + 1) * P],
                                      ident)
                mm.then_inc(s_pt, 1)
            pe.wait_ge(s_la, 16 * 2)
            pe.wait_ge(s_pin, 16 * (2 + KD))
            for j in range(2):
                for c in range(KD):
                    o = KD * D + j * D + c * P
                    mm = pe.transpose((p_lat, p_lbt)[j][:, c * P:(c + 1) * P], w_src[:, o:o + P], ident)
                mm.then_inc(s_pt, 1)

            def split_matmul(dst, lhs, rhs, n, stop):
                parts = [(k, a_, b_) for k in range(n) for a_, b_ in ((HI, HI), (HI, LO), (LO, HI))]
                for m, (k, a_, b_) in enumerate(parts):
                    mm = pe.matmul(dst, lhs(k, a_), rhs(k, b_), start=(m == 0), stop=(stop and m == len(parts) - 1))
                return mm

            def transpose_halves(dst, rows):
                for a_ in (HI, LO):
                    for k in range(KD):
                        mm = pe.transpose(dst[:, a_, k, :], rows[:, a_, k * P:(k + 1) * P], ident16[:, :])
                return mm

            def transpose_x(c, i):
                pe.wait_ge(s_xlo, tval(c, i, 2))
                if c >= 0:
                    pe.wait_ge(s_xt, tval(c, i, 1))
                transpose_halves(p_tx, x16).then_inc(s_tx, 1)

            def transpose_h(c, i):
                pe.wait_ge(s_hlo, tval(c, i))
                if c >= 2:
                    pe.wait_ge(s_ht, tval(c, i, -1))
                transpose_halves(p_th, h16).then_inc(s_th, 1)

            def router(c, i):
                pe.wait_ge(s_ht, tval(c, i, -1))
                if c >= 3:
                    pe.wait_ge(s_rlog, tval(c, i, -2))
                for k in range(KD):
                    for a_ in (HI, LO):
                        mm = pe.matmul(p_rt, xt[:, (c - 1) % 2, a_, k, :], wr[:, k, :, :].rearrange("p a e -> p (a e)"),
                                       start=(k == 0 and a_ == HI), stop=(k == KD - 1 and a_ == LO))
                mm.then_inc(s_rt, 1)

            def step(c, i=None):
                b = c % 2
                if 0 <= c + 1 < T:
                    transpose_x(c, i)
                if c == 0:
                    pe.wait_ge(s_plo, 2)
                if 0 <= c < T:
                    pe.wait_ge(s_xt, tval(c, i, 1))
                    if c >= 1:
                        pe.wait_ge(s_xam, tval(c, i))
                    split_matmul(p_xa, lambda k, a_: lat[:, k, a_, :], lambda k, b_: xt[:, b, b_, k, :],
                                 KD, True).then_inc(s_xa, 1)
                if c >= 2:
                    router(c, i)
                if 0 <= c < T:
                    if c == 0:
                        pe.wait_ge(s_plo, KD + 2)
                    if c == 1:
                        pe.wait_ge(s_phi, KD + 3)
                        pe.wait_ge(s_plo, KD + 3)
                    if c >= 2:
                        pe.wait_ge(s_hlo, tval(c, i, -1))
                    split_matmul(p_h[b], lambda k, a_: xt[:, b, a_, k, :], lambda k, b_: cw[:, k, b_, :], KD, False)
                if c == T - 1:
                    transpose_rows(0, None)
                if 0 <= c - 1 < T:
                    transpose_h(c, i)
                if 0 <= c < T:
                    if c == 0:
                        pe.wait_ge(s_phi, KD + 2)
                    pe.wait_ge(s_xam, tval(c, i, 1))
                    pe.matmul(p_h[b], xam[:, :], lbt[:, :], start=False, stop=True).then_inc(s_h, 1)

            def beside(c):
                if c == 3:
                    pe.wait_ge(s_m16, 1)
                    pe.wait_ge(s_const, 10)
                    pe.wait_ge(s_fht, 3)
                    pe.matmul(p_rank, upper16, m16, start=True, stop=True)
                    pe.matmul(p_count, ones16, m16, start=True, stop=True).then_inc(s_rmm, 1)
                if c == 4:
                    pe.wait_ge(s_rcp, 2)

            def transpose_rows(hc, i):
                hpar = hc % 2
                if hc < H1:
                    landed, count = s_hin, hc // 2 + 1
                elif hc < H2:
                    landed, count = s_hgat, (hc - H1) // 2 + 1
                else:
                    landed, count = s_hin, (H1 + 1 - hpar) // 2 + (hc - H2) // 2 + 1
                pe.wait_ge(landed[hpar], tval(count, i, 0, 1) * 16)
                transpose_halves(p_fth, hin[:, hpar, :, :]).then_inc(s_fth, 1)

            def weights(w, s, e, k, half):
                if s.shared:
                    return w[:, s.expert, k, half, :]
                return w[:, ds(e, 1), k, half, :].rearrange("p a n -> p (a n)")

            def expert_of(s):
                if s.shared:
                    return None
                o = etile[0:1, s.j:s.j + 1] if isinstance(s.j, int) else etile[0:1, ds(s.j, 1)]
                return pe.value_load(o, min_val=0, max_val=E - 1)

            def gate_up_high(s, e):
                pe.wait_ge(s_fht, s.h + 1)
                if s.c == 1:
                    pe.wait_ge(s_rlog, T)
                    pe.wait_ge(s_hlo, T)
                if s.c >= 2:
                    pe.wait_ge(s_silu, s.n - 1)
                    pe.wait_ge(s_a, s.n - 1)
                for k in range(KD):
                    for wh in (HI, LO):
                        for w, dst in ((wg, p_g), (wu, p_u)):
                            pe.matmul(dst[s.par], ht[s.hpar][:, HI, k, :], weights(w, s, e, k, wh),
                                      start=(k == 0 and wh == HI), stop=False)

            def gate_up_low(s, e):
                for k in range(KD):
                    for w, dst in ((wg, p_g), (wu, p_u)):
                        mm = pe.matmul(dst[s.par], ht[s.hpar][:, LO, k, :], weights(w, s, e, k, HI),
                                       start=False, stop=(k == KD - 1))
                mm.then_inc(s_gu, 1)

            def slot(s, prev):
                if s:
                    if s.c == N1:
                        pe.wait_ge(s_et, 1)
                    e = expert_of(s)
                    if s.last and s.c < NS - 1:
                        pe.wait_ge(s_fht, s.h + 1)
                        transpose_rows(s.hc + 1, s.i)
                    if s.c:
                        gate_up_high(s, e)
                if prev:
                    pe.wait_ge(s_alo, prev.n + 1)
                    if prev.c >= 1:
                        pe.wait_ge(s_at, prev.n)
                    for a_ in (HI, LO):
                        for k in range(KH):
                            m = P if k < KH - 1 else HR
                            mm = pe.transpose(p_at[0:m, a_, k, :], a16[:, a_, k * P:k * P + m], ident16[:, :])
                    mm.then_inc(s_ta, 1)
                if s and s.c:
                    gate_up_low(s, e)
                if prev:
                    e = expert_of(prev)
                    pe.wait_ge(s_at, prev.n + 1)
                    if 2 <= prev.c < N1 + 2:
                        pe.wait_ge(s_acc, prev.n - 1)
                    elif N1 + 2 <= prev.c < N2 + 2:
                        pe.wait_ge(s_y, prev.n - 1 - N1)
                    elif prev.c >= N2 + 2:
                        pe.wait_ge(s_acc, prev.n - 1 - ET)
                    parts = [(k, a_, b_) for k in range(KH) for a_, b_ in ((HI, HI), (HI, LO), (LO, HI))]
                    for m, (k, a_, b_) in enumerate(parts):
                        rows = P if k < KH - 1 else HR
                        mm = pe.matmul(p_y[prev.par], at[0:rows, prev.par, a_, k, :], weights(wd, prev, e, k, b_)[0:rows],
                                       start=(m == 0), stop=(m == len(parts) - 1))
                    mm.then_inc(s_dn, 1)

            for c in range(-1, 4):
                step(c)
            with pe.Fori(0, 4) as i:
                for c in range(4, 10):
                    step(c, i)
            for c in range(28, T):
                step(c)
            pe.wait_ge(s_hlo, T - 1)
            gate_up_high(Slot(0), None)
            router(T, None)
            transpose_h(T, None)
            gate_up_low(Slot(0), None)
            router(T + 1, None)
            run_slots(pe, slot, beside)
            tail(slot)


_INS = ['x', 'itok_B_0_6', 'L0_cond_W', 'L0_cond_A', 'L0_cond_Bm', 'L0_cond_scalings', 'L0_ffn_W_router',
        'L0_ffn_We_gate', 'L0_ffn_We_up', 'L0_ffn_We_down', 'L0_ffn_Ws_gate', 'L0_ffn_Ws_up', 'L0_ffn_Ws_down']
_OUTS = [((16, 256, 512), 'float32')]


def kernel(**inputs):
    import numpy as _np
    import concourse.bacc as _bacc
    from concourse import mybir as _mybir
    from concourse.bass_utils import run_bass_kernel_spmd as _run

    nc = _bacc.Bacc("TRN2", target_bir_lowering=False, num_devices=1)
    arrays, args = {}, []
    for name in _INS:
        a = _np.ascontiguousarray(inputs[name])
        arrays[f"in_{name}_dram"] = a
        args.append(nc.dram_tensor(f"in_{name}_dram", a.shape, _mybir.dt.from_np(a.dtype), kind="ExternalInput").ap())
    for i, (shape, dtype) in enumerate(_OUTS):
        dt = _mybir.dt.from_np(_np.dtype(dtype))
        args.append(nc.dram_tensor(f"out_{i}_dram", shape, dt, kind="ExternalOutput").ap())
    adaln_moe_kernel(nc, *args)
    r = _run(nc, [arrays], core_ids=[0])
    got = tuple(r.results[0][f"out_{i}_dram"] for i in range(len(_OUTS)))
    return got[0]
```
